# Optimizing a Trainium2 kernel written in Bass

```python
import numpy as np
import jax
import jax.numpy as jnp

def _softmax(x, axis=-1):
    return jax.nn.softmax(x, axis=axis)

def _gelu(x):
    return jax.nn.gelu(x, approximate=True)

def _silu(x):
    return jax.nn.silu(x)

def _sigmoid(x):
    return jax.nn.sigmoid(x)

def _layernorm(x, axis=-1, eps=1e-05):
    m = jnp.mean(x, axis=axis, keepdims=True)
    v = jnp.var(x, axis=axis, keepdims=True)
    return (x - m) / jnp.sqrt(v + eps)

def _scatter_add(tgt, idx, src, axis=0):
    return tgt.at[idx].add(src)

def _segment_sum(src, seg, n):
    return jax.ops.segment_sum(src, seg, n)
kernel_name = 'mk_seq_preln_d1_jaxref_r4_715302'

def setup_inputs(seed: int=0):
    np.random.seed(seed)
    _w = jnp.asarray

    def _L0_attn_setup():
        import jax, jax.numpy as jnp
        import numpy as np
        B, S, D = (2, 1024, 512)
        EPS = 1e-05

        def rmsnorm(h, scale, eps=EPS):
            hf = h.astype(jnp.float32)
            hf = hf * jax.lax.rsqrt(jnp.mean(hf * hf, axis=-1, keepdims=True) + eps)
            return hf.astype(h.dtype) * scale
        key = jax.random.key(seed)
        kx, kr, kf, kc, ko = jax.random.split(key, 5)
        sc = 1.0 / np.sqrt(D).astype(np.float32)
        return {'x': jax.random.normal(kx, (B, S, D), jnp.float32), 'Wr': jax.random.normal(kr, (D, D), jnp.float32) * sc, 'Wf': jax.random.normal(kf, (D, D), jnp.float32) * sc, 'Wc': jax.random.normal(kc, (D, D), jnp.float32) * sc, 'Wo': jax.random.normal(ko, (D, D), jnp.float32) * sc, 'ln_scale': jnp.ones((D,), jnp.float32)}
    _L0_attn_in = _L0_attn_setup()

    def _L0_ffn_setup():
        import jax, jax.numpy as jnp
        import numpy as np
        CAPACITY_FACTOR = 1.0

        def _top1_gate(x, w_gate):
            S, E = (x.shape[0], w_gate.shape[1])
            capacity = int(CAPACITY_FACTOR * S / E)
            logits = x @ w_gate
            gates = jax.nn.softmax(logits, axis=-1)
            idx1 = jnp.argmax(gates, axis=-1)
            mask1 = jax.nn.one_hot(idx1, E, dtype=gates.dtype)
            locations1 = jnp.cumsum(mask1, axis=0) - mask1
            mask1 = mask1 * (locations1 < capacity)
            locations1_s = jnp.sum(locations1 * mask1, axis=1).astype(jnp.int32)
            gates_masked = gates * mask1
            loc_oh = jax.nn.one_hot(locations1_s, capacity, dtype=gates.dtype) * jnp.sum(mask1, axis=1, keepdims=True)
            combine_weights = jnp.einsum('se,sc->sec', gates_masked, loc_oh)
            dispatch_mask = (combine_weights > 0).astype(gates.dtype)
            return (combine_weights, dispatch_mask)
        key = jax.random.key(seed)
        k1, k2, k3, k4 = jax.random.split(key, 4)
        B, T, D, E, F = (4, 512, 512, 8, 2048)
        hidden_states = jax.random.normal(k1, (B, T, D), dtype=jnp.float32)
        w_gate = jax.random.normal(k2, (D, E), dtype=jnp.float32) * 0.02
        w1 = jax.random.normal(k3, (E, D, F), dtype=jnp.float32) * 0.02
        w2 = jax.random.normal(k4, (E, F, D), dtype=jnp.float32) * 0.02
        return {'hidden_states': hidden_states, 'w_gate': w_gate, 'w1': w1, 'w2': w2}
    _L0_ffn_in = _L0_ffn_setup()
    _d = {'L0_attn_x': _L0_attn_in['x'], 'L0_attn_Wr': _L0_attn_in['Wr'], 'L0_attn_Wf': _L0_attn_in['Wf'], 'L0_attn_Wc': _L0_attn_in['Wc'], 'L0_attn_Wo': _L0_attn_in['Wo'], 'L0_attn_ln_scale': _L0_attn_in['ln_scale'], 'L0_ffn_w_gate': _L0_ffn_in['w_gate'], 'L0_ffn_w1': _L0_ffn_in['w1'], 'L0_ffn_w2': _L0_ffn_in['w2']}
    _x0 = _d['L0_attn_x']
    _d['L0_attn_x'] = jax.random.normal(jax.random.fold_in(jax.random.key(seed), 1), (2, 1024, 512), dtype=_x0.dtype)
    del _x0
    return _d

def reference(L0_attn_x, L0_attn_Wr, L0_attn_Wf, L0_attn_Wc, L0_attn_Wo, L0_attn_ln_scale, L0_ffn_w_gate, L0_ffn_w1, L0_ffn_w2):

    def _L0_attn_ref(x, Wr, Wf, Wc, Wo, ln_scale):
        import jax, jax.numpy as jnp
        import numpy as np
        B, S, D = (2, 1024, 512)
        EPS = 1e-05

        def rmsnorm(h, scale, eps=EPS):
            hf = h.astype(jnp.float32)
            hf = hf * jax.lax.rsqrt(jnp.mean(hf * hf, axis=-1, keepdims=True) + eps)
            return hf.astype(h.dtype) * scale
        r = jax.nn.silu(x @ Wr)
        f = jax.nn.sigmoid(x @ Wf)
        c = jax.nn.silu(x @ Wc)

        def combine(a, b):
            fa, ca = a
            fb, cb = b
            return (fa * fb, fb * ca + (1.0 - fb) * cb)
        _, h = jax.lax.associative_scan(combine, (f, c), axis=1)
        y = r * rmsnorm(h, ln_scale) @ Wo
        return y

    def _L0_ffn_ref(hidden_states, w_gate, w1, w2):
        import jax, jax.numpy as jnp
        import numpy as np
        CAPACITY_FACTOR = 1.0

        def _top1_gate(x, w_gate):
            S, E = (x.shape[0], w_gate.shape[1])
            capacity = int(CAPACITY_FACTOR * S / E)
            logits = x @ w_gate
            gates = jax.nn.softmax(logits, axis=-1)
            idx1 = jnp.argmax(gates, axis=-1)
            mask1 = jax.nn.one_hot(idx1, E, dtype=gates.dtype)
            locations1 = jnp.cumsum(mask1, axis=0) - mask1
            mask1 = mask1 * (locations1 < capacity)
            locations1_s = jnp.sum(locations1 * mask1, axis=1).astype(jnp.int32)
            gates_masked = gates * mask1
            loc_oh = jax.nn.one_hot(locations1_s, capacity, dtype=gates.dtype) * jnp.sum(mask1, axis=1, keepdims=True)
            combine_weights = jnp.einsum('se,sc->sec', gates_masked, loc_oh)
            dispatch_mask = (combine_weights > 0).astype(gates.dtype)
            return (combine_weights, dispatch_mask)
        B, T, D = hidden_states.shape
        x = hidden_states.reshape(-1, D)
        combine_weights, dispatch_mask = _top1_gate(x, w_gate)
        dispatched = jnp.einsum('sec,sm->ecm', dispatch_mask, x)
        h = jax.nn.gelu(jnp.einsum('ecd,edf->ecf', dispatched, w1))
        expert_out = jnp.einsum('ecf,efd->ecd', h, w2)
        combined = jnp.einsum('sec,ecm->sm', combine_weights, expert_out)
        return combined.reshape(B, T, D)
    x = L0_attn_x
    x = x + _L0_attn_ref(_layernorm(x, axis=-1), L0_attn_Wr, L0_attn_Wf, L0_attn_Wc, L0_attn_Wo, L0_attn_ln_scale)
    x = x + _L0_ffn_ref(_layernorm(x, axis=-1), L0_ffn_w_gate, L0_ffn_w1, L0_ffn_w2)
    return x

_drawn_inputs = setup_inputs


def setup_inputs(seed=0):
    import zlib

    import numpy as np

    out = dict(_drawn_inputs(seed))
    spreads = {'L0_attn_ln_scale': (1.0, 0.2)}
    factors = {}
    for name, (base, spread) in spreads.items():
        noise = np.random.default_rng([zlib.crc32(name.encode()), seed]).standard_normal(out[name].shape)
        drawn = base * np.exp(spread * noise) if base else spread * noise
        out[name] = jnp.asarray(drawn.astype(out[name].dtype))
    for name, factor in factors.items():
        out[name] = (out[name] * factor).astype(out[name].dtype)
    return out
```

```python
from contextlib import ExitStack

import concourse.bass as bass
from concourse import mybir

P = 128
F32 = mybir.dt.float32
F16 = mybir.dt.float16
U32 = mybir.dt.uint32
ALU = mybir.AluOpType
ACT = mybir.ActivationFunctionType
AX_X = mybir.AxisListType.X

EPS = 1e-5
WSCALE = 64.0
UNSCALE = WSCALE**-2
HI, LO = 0, 1
PASSES = ((HI, HI), (HI, LO), (LO, HI))


class Chain:

    def __init__(self, sem, engine, per_unit):
        self.sem, self.engine, self.per_unit, self.done = sem, engine, per_unit, 0

    def start(self, unit):
        self.base, self.done = unit * self.per_unit, 0

    def step(self, instruction):
        instruction.then_inc(self.sem, 1)
        self.done += 1
        return self.base + self.done

    def after(self, value):
        self.engine.wait_ge(self.sem, value)

    def link(self, instruction):
        self.after(self.step(instruction))

    def end(self):
        assert self.done == self.per_unit, (self.sem, self.done)


def recurrent_block_with_experts(nc, x, Wr, Wf, Wc, Wo, ln_scale, w_gate, w1, w2, out):
    B, S, D = x.shape
    E, _, F = w1.shape
    TOK = B * S
    CAP = TOK // E
    CH = 512
    NCH = TOK // CH
    TPC = CH // P
    NT = TOK // P
    KD = D // P
    NP = F // 256
    CT = CAP // P
    RING = 8
    AW = 4
    XW = D + 4
    MEAN, RSTD, GATE, ID = D, D + 1, D + 2, D + 3
    NOWHERE = 1 << 20
    TREE = 3 * 9 + 3 * 10 - 1
    assert AW * KD * D == RING * 1024 and NP == RING and KD * 256 == 1024 and S % CH == 0 and CT == 2
    CHUNKS_PER_SEQ = S // CH
    assert CHUNKS_PER_SEQ == 2

    x_rows = x.rearrange("b s d -> (b s) d")
    out_rows = out.rearrange("b s d -> (b s) d")
    x_tiles = x_rows.rearrange("(t p) d -> p t d", p=P)
    out_tiles = out_rows.rearrange("(t p) d -> p t d", p=P)
    table = nc.dram_tensor("expert_rows", (E * CAP, XW), F32, kind="Internal").ap()
    table_tiles = table.rearrange("(t p) d -> p t d", p=P)
    w1_chunks = w1.rearrange("e (k p) (j n) -> e j p k n", p=P, j=NP)
    w2_chunks = w2.rearrange("e (j a p) n -> e j p a n", p=P, j=NP)

    with ExitStack() as ctx:
        def sb(name, shape, dt=F32):
            return ctx.enter_context(nc.sbuf_tensor(name, shape, dt))

        def sem(name):
            return ctx.enter_context(nc.semaphore(name))

        rows = sb("rows", [P, NT, XW])
        raw = sb("raw", [P, RING, 1024])
        wB = [sb("wB_hi", [P, RING * 1024], F16), sb("wB_lo", [P, RING * 1024], F16)]
        wA = [sb("wA_hi", [P, RING * 1024], F16), sb("wA_lo", [P, RING * 1024], F16)]
        proj = [w[:].rearrange("p (w k n) -> p w k n", w=AW, k=KD) for w in wB]
        w2s = [w[:].rearrange("p (j a n) -> p j a n", j=NP, a=2) for w in wB]
        w1s = [w[:].rearrange("p (j k n) -> p j k n", j=NP, k=KD) for w in wA]
        xT = sb("xT", [P, 2, 2, KD, CH], F16)
        xTe = xT[:, 0].rearrange("p h k n -> p (h k n)")[:, 0:2 * KD * CAP].rearrange("p (h k n) -> p h k n", h=2, k=KD)
        f_all = wA[HI][:].bitcast(F32).rearrange("p (c m n) -> p c m n", c=2, m=KD)
        r_all = wA[LO][:].bitcast(F32).rearrange("p (c m n) -> p c m n", c=2, m=KD)
        state = sb("state", [P, 2, KD, 1 + CH])
        hid = state[:].rearrange("p c m n -> p (c m n)").bitcast(F16)[:, 0:2 * F // P * CAP].rearrange("p (h f n) -> p h f n", h=2, n=CAP)
        tmp = sb("tmp", [P, KD, CH // 2])
        gel = tmp[:].rearrange("p m n -> p (m n)").rearrange("p (b n) -> p b n", b=2)
        hsq = sb("hsq", [P, KD, CH])
        pT = [sb("pT_hi", [P, KD, CH], F16), sb("pT_lo", [P, KD, CH], F16)]
        done_rows = hsq[:, 0:2, :]
        xn = sb("xn", [P, 2, D])
        xs = sb("xs", [P, TPC, 2, D], F16)
        x1n = sb("x1n", [P, TPC, D])
        x1T = sb("x1T", [P, 2, KD, P])
        fill = x1T[:].rearrange("p b k n -> p (b k n)")[:, 0:XW]
        ident = sb("ident", [P, P], F16)
        ident32 = sb("ident32", [P, P])
        earlier = sb("earlier", [P, P], F16)
        ones16 = sb("ones16", [P, P], F16)
        ones32 = sb("ones32", [P, 1])
        neg_half = sb("neg_half", [P, TPC])
        rank = sb("rank", [P, TPC, E])
        scale64 = sb("scale64", [P, KD])
        scale_in = sb("scale_in", [P, KD])
        wg_in = sb("wg_in", [P, KD, E])
        keep = sb("keep", [P, NCH])
        st = {n: sb(f"st_{n}", [P, TPC, 6]) for n in "tb"}
        mv = {n: sb(f"mv_{n}", [P, TPC, 2]) for n in "tb"}
        ve = {n: sb(f"ve_{n}", [P, TPC]) for n in "tbr"}
        neg_mean = {n: sb(f"neg_mean_{n}", [P, TPC]) for n in "tb"}
        shift = {n: sb(f"shift_{n}", [P, TPC]) for n in "tb"}
        rs = {n: sb(f"rs_{n}", [P, TPC]) for n in "tbr"}
        small = {n: sb(f"sm_{n}", [P, TPC, E]) for n in ("lg", "d", "sg", "om", "rc", "eq")}
        small["ex"], small["pm"] = small["om"], small["lg"]
        col = {n: sb(f"col_{n}", [P, TPC]) for n in ("max", "sum", "gate", "m8", "pos", "slot", "over", "where")}
        onehot = sb("onehot", [P, TPC, E], F16)
        before = sb("before", [P, TPC + 1, E], F16)
        slot_ids = sb("slot_ids", [P, NT], U32)
        row_ids = sb("row_ids", [P, CT], U32)

        def bank(name, n, dt=F32):
            return ctx.enter_context(nc.psum_tensor(name, [P, n, 2048 // (4 if dt == F32 else 2)], dt))

        zps = bank("zps", 3)
        sps = bank("sps", 1)
        tps = bank("tps", 2, F16)
        wps = bank("wps", 2)
        tps16 = tps[:].rearrange("p b (h k n) -> p b h k n", h=2, k=KD)
        tps32 = tps[:].bitcast(F32).rearrange("p b (k n) -> p b k n", k=KD)

        x_first, x_rest, small_in = sem("x_first"), sem("x_rest"), sem("small_in")
        raw_in = [sem(f"raw_in{i}") for i in range(RING)]
        hi_split, lo_split = sem("hi_split"), sem("lo_split")
        small_split = sem("small_split")
        consts, setup = sem("consts"), sem("setup")
        table_clear, scattered, base_out = sem("table_clear"), sem("scattered"), sem("base_out")
        nrm = {p: {n: sem(f"{p}_{n}") for n in ("var", "rstd", "xn", "hi", "lo", "turned", "copied")} for p in "tbe"}
        chain_s, chain_g = sem("chain_s"), sem("chain_g")
        zf_done, zc_done, zr_done = sem("zf_done"), sem("zc_done"), sem("zr_done")
        tanh_ready, f_ready, c_ready, r_ready = sem("tanh_ready"), sem("f_ready"), sem("c_ready"), sem("r_ready")
        f_products, tree_step, states_ready, hsq_ready, phi_ready, p_ready, plo_ready = (
            sem(n) for n in ("f_products", "tree_step", "states_ready", "hsq_ready", "phi_ready", "p_ready", "plo_ready"))
        rms_done, rms_var, rms_rstd, wo_done, x1_ready = (sem(n) for n in ("rms_done", "rms_var", "rms_rstd", "wo_done", "x1_ready"))
        logits_done, diff_ready, sig_ready, onehot_ready, pos_done, slots_ready = (
            sem(n) for n in ("logits_done", "diff_ready", "sig_ready", "onehot_ready", "pos_done", "slots_ready"))
        e_first, e_rest = sem("e_first"), sem("e_rest")
        up_done, gel_ready, hhi_ready, hlo_ready, down_done = (sem(n) for n in ("up_done", "gel_ready", "hhi_ready", "hlo_ready", "down_done"))
        ids_ready, combined, rows_out = sem("ids_ready"), sem("combined"), [sem(f"rows_out{t}") for t in range(CT)]

        block = ctx.enter_context(nc.Block())

        def wait(eng, s, value):
            if not isinstance(value, int) or value > 0:
                eng.wait_ge(s, value)

        def two_before(count, t):
            return count + max(t - 1, 0)

        def xs_slot(part, t):
            return t if part == "b" else t % 2

        def first(unit):
            return isinstance(unit, int) and unit == 0

        def tile_at(t):
            return rows[:, bass.ds(t, 1), :].rearrange("p a d -> p (a d)")

        def splits_before(e, matrix):
            return RING * (1 + 2 * e + (matrix == "w2"))

        def raw_wait(eng, e, matrix, j):
            eng.wait_ge(raw_in[j], 16 * (splits_before(e, matrix) // RING + 1) if isinstance(e, int)
                        else 32 * e + (48 if matrix == "w2" else 32))

        @block.sync
        def _(sp):
            sp.dma_start(rows[:, 0:TPC, 0:D], x_tiles[:, 0:TPC, :]).then_inc(x_first, 16)
            for i, w in enumerate((Wf, Wc, Wr, Wo)):
                w_in = w.rearrange("(k p) n -> p k n", p=P)
                for half in range(2):
                    sp.dma_start(raw[:, 2 * i + half, :].rearrange("p (k n) -> p k n", k=2),
                                 w_in[:, 2 * half:2 * half + 2, :]).then_inc(raw_in[2 * i + half], 16)
                if i == 0:
                    with nc.allow_non_contiguous_dma(reason="2 KB in all"):
                        sp.dma_start(scale_in[:], ln_scale.rearrange("(k p) -> p k", p=P)).then_inc(small_in, 16)
                    sp.dma_start(wg_in[:], w_gate.rearrange("(k p) e -> p k e", p=P)).then_inc(small_in, 16)
                if i == 2:
                    sp.dma_start(rows[:, TPC:NT, 0:D], x_tiles[:, TPC:NT, :]).then_inc(x_rest, 16)
            sp.wait_ge(consts, 1)
            for t in range(NT):
                sp.dma_start(table_tiles[:, t, :], fill).then_inc(table_clear, 16)

            def load(e, matrix):
                for j in range(NP):
                    sp.wait_ge(lo_split, splits_before(e, matrix) - RING + j + 1)
                    if matrix == "w1":
                        src = w1_chunks[bass.ds(e, 1), j].rearrange("e p k n -> p (e k) n")
                        dst = raw[:, j, :].rearrange("p (k n) -> p k n", k=KD)
                    else:
                        src = w2_chunks[bass.ds(e, 1), j].rearrange("e p a n -> p (e a) n")
                        dst = raw[:, j, :].rearrange("p (a n) -> p a n", a=2)
                    sp.dma_start(dst, src).then_inc(raw_in[j], 16)

            load(0, "w1")
            load(0, "w2")
            sp.wait_ge(scattered, 16 * NT)
            sp.wait_ge(base_out, 16 * NCH)
            sp.dma_start(rows[:, 0:CT, :], table_tiles[:, 0:CT, :]).then_inc(e_first, 16)
            sp.dma_start(rows[:, CT:NT, :], table_tiles[:, CT:NT, :]).then_inc(e_rest, 16)
            with sp.Fori(1, E) as e:
                load(e, "w1")
                load(e, "w2")

        @block.gpsimd
        def _(pool):
            steps = [0]

            def made(instruction):
                steps[0] += 1
                instruction.then_inc(setup, 1)
                return steps[0]

            made(nc.gpsimd.memset(fill, 0.0))
            made(nc.gpsimd.memset(ident[:], 1.0))
            made(nc.gpsimd.memset(earlier[:], 1.0))
            made(nc.gpsimd.memset(ones16[:], 1.0))
            made(nc.gpsimd.memset(ones32[:], 1.0))
            made(nc.gpsimd.memset(neg_half[:], -0.5))
            made(nc.gpsimd.memset(state[:, 0, :, 0:1], 0.0))
            made(nc.gpsimd.memset(ident32[:], 1.0))
            made(nc.gpsimd.memset(keep[:], 1.0))
            made(nc.gpsimd.memset(before[:], 0.0))
            pool.wait_ge(setup, steps[0])
            made(nc.gpsimd.iota(fill[:, ID:ID + 1].bitcast(U32), pattern=[[0, 1]], base=NOWHERE, channel_multiplier=0))
            for e in range(E):
                made(nc.gpsimd.memset(rank[:, :, e], float(E - e)))
            for c in range(0, NCH, CHUNKS_PER_SEQ):
                made(nc.gpsimd.memset(keep[:, c:c + 1], 0.0))
            made(nc.gpsimd.affine_select(out=ident[:], in_=ident[:], compare_op=ALU.is_equal, fill=0.0,
                                         base=0, pattern=[[-1, P]], channel_multiplier=1))
            made(nc.gpsimd.affine_select(out=ident32[:], in_=ident32[:], compare_op=ALU.is_equal, fill=0.0,
                                         base=0, pattern=[[-1, P]], channel_multiplier=1))
            made(nc.gpsimd.affine_select(out=earlier[:], in_=earlier[:], compare_op=ALU.is_gt, fill=0.0,
                                         base=0, pattern=[[1, P]], channel_multiplier=-1))
            pool.wait_ge(setup, steps[0])
            for t in range(NT):
                made(nc.gpsimd.iota(rows[:, t, ID:ID + 1].bitcast(U32), pattern=[[0, 1]], base=t * P, channel_multiplier=1))
            pool.wait_ge(setup, steps[0])
            nc.gpsimd.memset(slot_ids[:], 0).then_inc(consts, 1)

            def power(part, c):
                pool.wait_ge(nrm[part]["var"], c + 1)
                made(nc.gpsimd.tensor_tensor(rs[part][:], ve[part][:], neg_half[:], ALU.pow))
                pool.wait_ge(setup, steps[0])
                nc.gpsimd.tensor_tensor(shift[part][:], neg_mean[part][:], rs[part][:], ALU.mult).then_inc(nrm[part]["rstd"], 1)

            def part_b_norms(c):
                pool.wait_ge(rms_var, c + 1)
                nc.gpsimd.tensor_tensor(rs["r"][:], ve["r"][:], neg_half[:], ALU.pow).then_inc(rms_rstd, 1)
                power("b", c)
                pool.wait_ge(x1_ready, TPC * (c + 1))
                pool.dma_start(out_tiles[:, TPC * c:TPC * c + TPC, :], rows[:, TPC * c:TPC * c + TPC, 0:D]).then_inc(base_out, 16)

            def scatter(c):
                pool.wait_ge(slots_ready, c + 1)
                if c == 0:
                    pool.wait_ge(table_clear, 16 * NT)
                for t in range(TPC * c, TPC * c + TPC):
                    pool.indirect_dma_start(
                        out=table, out_offset=bass.IndirectOffsetOnAxis(ap=slot_ids[:, t:t + 1], axis=0),
                        in_=rows[:, t, :], in_offset=None, bounds_check=E * CAP - 1, oob_is_err=False).then_inc(scattered, 16)

            power("t", 0)
            power("t", 1)
            for c in range(NCH):
                if c + 2 <= NCH:
                    power("t", c + 2)
                part_b_norms(c)
                scatter(c)

            for e in range(E):
                for t in range(CT):
                    pool.wait_ge(combined, CT * e + t + 1)
                    pool.indirect_dma_start(
                        out=out_rows, out_offset=bass.IndirectOffsetOnAxis(ap=row_ids[:, t:t + 1], axis=0),
                        in_=done_rows[:, t, :], in_offset=None, bounds_check=TOK - 1, oob_is_err=False).then_inc(rows_out[t], 16)
            for t in range(CT):
                pool.wait_ge(rows_out[t], 16 * E)

        @block.scalar
        def _(act):
            def attn_weights(n):
                act.wait_ge(raw_in[n], 16)
                nc.scalar.activation(wB[HI][:, 1024 * n:1024 * n + 1024], raw[:, n, :], ACT.Copy, scale=WSCALE).then_inc(hi_split, 1)

            def normal(u, src):
                for t in range(TPC):
                    if t == 0:
                        act.wait_ge(nrm["t"]["rstd"], u + 1)
                        wait(act, nrm["t"]["turned"], TPC * u)
                    wait(act, nrm["t"]["lo"], two_before(TPC * u, t))
                    for dst in (xn[:, t % 2, :], xs[:, t, HI, :]):
                        last = nc.scalar.activation(dst, src(t), ACT.Identity, scale=rs["t"][:, t:t + 1], bias=shift["t"][:, t:t + 1])
                    last.then_inc(nrm["t"]["hi"], 1)

            def normal_x1(c):
                for t in range(TPC):
                    if t == 0:
                        act.wait_ge(nrm["b"]["rstd"], c + 1)
                        wait(act, nrm["b"]["turned"], TPC * c)
                    nc.scalar.activation(x1n[:, t, :], tile_at(TPC * c + t)[:, 0:D], ACT.Identity, scale=rs["b"][:, t:t + 1],
                                         bias=shift["b"][:, t:t + 1]).then_inc(nrm["b"]["xn"], 1)

            def copy_turned(part, u, tiles, dst, src):
                for t in range(tiles):
                    act.wait_ge(nrm[part]["turned"], tiles * u + t + 1)
                    nc.scalar.activation(dst(t), src[:, t % 2], ACT.Copy).then_inc(nrm[part]["copied"], 1)

            def t_copies(c):
                wait(act, zr_done, 4 * (c - 1))
                copy_turned("t", c, TPC, lambda t: xT[:, bass.ds(c & 1, 1), :, :, t * P:(t + 1) * P].rearrange("p c h k n -> p (c h) k n"), tps16)

            def of_chunk(a, c, m):
                return a[:, bass.ds(c & 1, 1), m, :].rearrange("p c n -> p (c n)")

            def gates(c, m):
                act.wait_ge(zf_done, 4 * c + m + 1)
                if m == 0:
                    wait(act, p_ready, 4 * (c - 1))
                    wait(act, plo_ready, 4 * (c - 1))
                nc.scalar.activation(zps[:, 0, :], zps[:, 0, :], ACT.Tanh, scale=UNSCALE / 2).then_inc(tanh_ready, 1)
                act.wait_ge(zc_done, 4 * c + m + 1)
                nc.scalar.activation(of_chunk(state, c, m)[:, 1:1 + CH], zps[:, 1, :], ACT.Silu, scale=UNSCALE).then_inc(c_ready, 1)
                act.wait_ge(tanh_ready, 4 * c + m + 1)
                nc.scalar.activation(of_chunk(f_all, c, m), zps[:, 0, :], ACT.Copy, scale=0.5, bias=0.5).then_inc(f_ready, 1)
                act.wait_ge(zr_done, 4 * c + m + 1)
                nc.scalar.activation(of_chunk(r_all, c, m), zps[:, 2, :], ACT.Silu, scale=UNSCALE).then_inc(r_ready, 1)

            def squares(c):
                act.wait_ge(states_ready, c + 1)
                wait(act, rms_done, c)
                for m in range(KD):
                    nc.scalar.activation(hsq[:, m, :], of_chunk(state, c, m)[:, 1:1 + CH], ACT.Square).then_inc(hsq_ready, 1)

            def p_hi(c):
                for m in range(KD):
                    act.wait_ge(p_ready, 4 * c + m + 1)
                    if m == 0:
                        wait(act, wo_done, TPC * c)
                    nc.scalar.activation(pT[HI][:, m, :], of_chunk(r_all, c, m), ACT.Copy).then_inc(phi_ready, 1)

            def tanh_of_diff(c):
                act.wait_ge(diff_ready, c + 1)
                nc.scalar.activation(small["sg"][:], small["d"][:], ACT.Tanh, scale=0.5 / WSCALE).then_inc(sig_ready, 1)

            def x_tile(c):
                return lambda t: rows[:, TPC * c + t, 0:D] if isinstance(c, int) else tile_at(TPC * (c & (NCH - 1)) + t)[:, 0:D]

            def body(a, b, t):
                if a is not None:
                    gates(a, 0)
                    gates(a, 1)
                if b is not None:
                    squares(b)
                    p_hi(b)
                if a is not None:
                    gates(a, 2)
                if t is not None:
                    normal(t, x_tile(t))
                    t_copies(t)
                if a is not None:
                    gates(a, 3)
                if b is not None:
                    normal_x1(b)
                    copy_turned("b", b, TPC, lambda t: x1T[:, t % 2], tps32)
                    tanh_of_diff(b)

            def w1_hi(e):
                for j in range(NP):
                    raw_wait(act, e, "w1", j)
                    if j == 0:
                        wait(act, up_done, NP * e)
                        act.wait_ge(plo_ready, KD * NCH)
                    nc.scalar.activation(wA[HI][:, 1024 * j:1024 * j + 1024], raw[:, j, :], ACT.Copy, scale=WSCALE).then_inc(hi_split, 1)

            def expert_hi(e):
                for t in range(CT):
                    act.wait_ge(nrm["e"]["xn"], CT * e + t + 1)
                    if t == 0:
                        act.wait_ge(nrm["t"]["turned"], TPC * (NCH + 1))
                        wait(act, nrm["e"]["turned"], CT * e)
                    nc.scalar.activation(xs[:, t, HI, :], xn[:, t, :], ACT.Copy).then_inc(nrm["e"]["hi"], 1)

            normal(0, x_tile(0))
            for n in range(6):
                attn_weights(n)
            t_copies(0)
            attn_weights(6)
            attn_weights(7)
            normal(1, x_tile(1))
            t_copies(1)
            body(0, None, None)
            act.wait_ge(table_clear, 16 * NT)
            with act.Fori(1, NCH) as c:
                body(c, c - 1, c + 1)
            body(None, NCH - 1, None)
            w1_hi(0)

            def e_copies(e):
                copy_turned("e", e, CT, lambda t: xTe[:, :, :, t * P:(t + 1) * P], tps16)

            def expert(e, last):
                for j in range(NP):
                    act.wait_ge(up_done, NP * e + j + 1)
                    wait(act, hlo_ready, NP * e + j - 1)
                    nc.scalar.activation(gel[:, j % 2, :], zps[:, j % 3, :], ACT.Gelu_apprx_tanh, scale=UNSCALE).then_inc(gel_ready, 1)
                    raw_wait(act, e, "w2", j)
                    if j == 0:
                        wait(act, down_done, CT * e)
                        act.wait_ge(wo_done, NT)
                    nc.scalar.activation(wB[HI][:, 1024 * j:1024 * j + 1024], raw[:, j, :], ACT.Copy, scale=WSCALE).then_inc(hi_split, 1)
                if last:
                    return
                expert_hi(e + 1)
                act.wait_ge(up_done, NP * (e + 1))
                e_copies(e + 1)
                w1_hi(e + 1)

            expert_hi(0)
            e_copies(0)
            expert(0, False)
            with act.Fori(1, E - 1) as e:
                expert(e, False)
            expert(E - 1, True)

        @block.vector
        def _(dve):
            cs = Chain(chain_s, dve, 2)
            cg = Chain(chain_g, dve, 24)

            def split_lo(hi, lo, src, count):
                dve.wait_ge(hi_split, count)
                nc.vector.scalar_tensor_tensor(out=lo, in0=src, scalar=WSCALE, in1=hi, op0=ALU.mult, op1=ALU.subtract).then_inc(lo_split, 1)

            def attn_weights(n):
                split_lo(wB[HI][:, 1024 * n:1024 * n + 1024], wB[LO][:, 1024 * n:1024 * n + 1024], raw[:, n, :], n + 1)

            def statistics(part, source):
                for t in range(TPC):
                    nc.vector.bn_stats(st[part][:, t, :], source(t))
                nc.vector.drain()
                for t in range(TPC):
                    nc.vector.bn_aggr(mv[part][:, t, :], st[part][:, t, :])
                nc.vector.drain()
                nc.vector.tensor_scalar(neg_mean[part][:], mv[part][:, :, 0], -1.0, None, ALU.mult)
                nc.vector.tensor_scalar(ve[part][:], mv[part][:, :, 1], EPS, UNSCALE, ALU.add, ALU.mult).then_inc(nrm[part]["var"], 1)

            def t_statistics(c):
                statistics("t", lambda t: rows[:, TPC * c + t, 0:D] if isinstance(c, int) else tile_at(TPC * (c & (NCH - 1)) + t)[:, 0:D])

            def t_lo(c):
                for t in range(TPC):
                    dve.wait_ge(nrm["t"]["hi"], TPC * c + t + 1)
                    nc.vector.tensor_tensor(xs[:, t, LO, :], xn[:, t % 2, :], xs[:, t, HI, :], ALU.subtract).then_inc(nrm["t"]["lo"], 1)

            def recurrence(c):
                f_c = f_all[:, bass.ds(c & 1, 1)].rearrange("p c m n -> p (c m) n")
                s_c = state[:, bass.ds(c & 1, 1)].rearrange("p c m n -> p (c m) n")
                s_next = state[:, bass.ds((c + 1) & 1, 1)].rearrange("p c m n -> p (c m) n")
                cs.start(c)
                dve.wait_ge(f_ready, 4 * (c + 1))
                dve.wait_ge(c_ready, 4 * (c + 1))
                cs.link(nc.vector.tensor_tensor(f_c[:, :, 0:1], f_c[:, :, 0:1], keep[:, bass.ds(c, 1)].unsqueeze(1).to_broadcast([P, KD, 1]), ALU.mult))
                step = [0]

                def link(instruction):
                    instruction.then_inc(tree_step, 1)
                    step[0] += 1
                    dve.wait_ge(tree_step, TREE * c + step[0])

                g = 2
                while g <= CH:
                    n = CH // g
                    blocks = s_c[:, :, 1:1 + CH].rearrange("p m (i g) -> p m i g", g=g)
                    f_blocks = f_c.rearrange("p m (i g) -> p m i g", g=g)
                    c_left, c_right = blocks[:, :, :, g // 2 - 1], blocks[:, :, :, g - 1]
                    f_left, f_right = f_blocks[:, :, :, g // 2 - 1], f_blocks[:, :, :, g - 1]
                    t_g = tmp[:, :, 0:n]
                    link(nc.vector.tensor_tensor(t_g, c_left, c_right, ALU.subtract))
                    link(nc.vector.tensor_tensor(t_g, t_g, f_right, ALU.mult))
                    nc.vector.tensor_tensor(f_right, f_right, f_left, ALU.mult)
                    link(nc.vector.tensor_tensor(c_right, c_right, t_g, ALU.add))
                    g *= 2
                while g >= 2:
                    n = max(CH // g, 1)
                    if g > CH:
                        c_here, f_here, h_before = s_c[:, :, CH:CH + 1], f_c[:, :, CH - 1:CH], s_c[:, :, 0:1]
                    else:
                        c_here = s_c[:, :, 1:1 + CH].rearrange("p m (i g) -> p m i g", g=g)[:, :, :, g // 2 - 1]
                        f_here = f_c.rearrange("p m (i g) -> p m i g", g=g)[:, :, :, g // 2 - 1]
                        h_before = s_c[:, :, 0:CH].rearrange("p m (i g) -> p m i g", g=g)[:, :, :, 0]
                    t_g = tmp[:, :, 0:n]
                    link(nc.vector.tensor_tensor(t_g, h_before, c_here, ALU.subtract))
                    link(nc.vector.tensor_tensor(t_g, t_g, f_here, ALU.mult))
                    last = nc.vector.tensor_tensor(c_here, c_here, t_g, ALU.add)
                    if g > 2:
                        link(last)
                    else:
                        last.then_inc(states_ready, 1)
                    g //= 2
                assert step[0] == TREE
                dve.wait_ge(states_ready, c + 1)
                cs.link(nc.vector.tensor_copy(s_next[:, :, 0:1], s_c[:, :, CH:CH + 1]))

            def gated(c):
                for m in range(KD + 1):
                    if m < KD:
                        if m == 0:
                            dve.wait_ge(r_ready, 4 * (c + 1))
                        r = r_all[:, bass.ds(c & 1, 1), m, :].rearrange("p c n -> p (c n)")
                        h = state[:, bass.ds(c & 1, 1), m, 1:1 + CH].rearrange("p c n -> p (c n)")
                        nc.vector.scalar_tensor_tensor(out=r, in0=h, scalar=scale64[:, m:m + 1], in1=r, op0=ALU.mult, op1=ALU.mult).then_inc(p_ready, 1)
                    if m >= 1:
                        dve.wait_ge(phi_ready, 4 * c + m)
                        r = r_all[:, bass.ds(c & 1, 1), m - 1, :].rearrange("p c n -> p (c n)")
                        nc.vector.tensor_tensor(pT[LO][:, m - 1, :], r, pT[HI][:, m - 1, :], ALU.subtract).then_inc(plo_ready, 1)

            def part_b_norms(c):
                dve.wait_ge(rms_done, c + 1)
                cg.start(c)
                cg.link(nc.vector.tensor_scalar(col["sum"][:], sps[:, 0, 0:TPC], 1.0 / D, EPS, ALU.mult, ALU.add))
                nc.vector.tensor_scalar(ve["r"][:], col["sum"][:], UNSCALE**-2, None, ALU.mult).then_inc(rms_var, 1)
                dve.wait_ge(rms_rstd, c + 1)
                src = lambda t: tile_at(TPC * c + t)[:, 0:D]
                for t in range(TPC):
                    dve.wait_ge(wo_done, TPC * c + t + 1)
                    nc.vector.scalar_tensor_tensor(out=src(t), in0=wps[:, t % 2, :], scalar=rs["r"][:, t:t + 1], in1=src(t),
                                                   op0=ALU.mult, op1=ALU.add).then_inc(x1_ready, 1)
                nc.vector.drain()
                statistics("b", src)
                cg.step(nc.vector.tensor_copy(payload(c, MEAN), mv["b"][:, :, 0]))
                dve.wait_ge(nrm["b"]["rstd"], c + 1)
                cg.step(nc.vector.tensor_copy(payload(c, RSTD), rs["b"][:]))

            def payload(c, what):
                return rows[:, bass.ds(TPC * c, TPC), what]

            def each(a):
                return a[:].unsqueeze(2).to_broadcast([P, TPC, E])

            def route(c):
                d, eq = small["d"], small["eq"]
                dve.wait_ge(logits_done, c + 1)
                cg.link(nc.vector.tensor_copy(small["lg"][:], sps[:, 0, 32:32 + TPC * E].rearrange("p (t e) -> p t e", e=E)))
                cg.link(nc.vector.tensor_reduce(col["max"][:], small["lg"][:], AX_X, ALU.max))
                nc.vector.tensor_tensor(d[:], small["lg"][:], each(col["max"]), ALU.subtract).then_inc(diff_ready, 1)
                dve.wait_ge(diff_ready, c + 1)
                cg.link(nc.vector.scalar_tensor_tensor(out=eq[:], in0=d[:], scalar=0.0, in1=rank[:], op0=ALU.is_ge, op1=ALU.mult))
                cg.link(nc.vector.tensor_reduce(col["m8"][:], eq[:], AX_X, ALU.max))
                cg.link(nc.vector.tensor_tensor(onehot[:], rank[:], each(col["m8"]), ALU.is_equal))
                cg.link(nc.vector.tensor_copy(before[:, 0, :], before[:, TPC, :]))
                for t in range(TPC - 1):
                    cg.link(nc.vector.tensor_tensor(before[:, t + 1, :], before[:, t, :], onehot[:, t, :], ALU.add))
                nc.vector.tensor_tensor(before[:, TPC, :], before[:, TPC - 1, :], onehot[:, TPC - 1, :], ALU.add).then_inc(onehot_ready, 1)

            def place(c):
                sg, om, rc, ex, pm = (small[n] for n in ("sg", "om", "rc", "ex", "pm"))
                dve.wait_ge(sig_ready, c + 1)
                cg.link(nc.vector.tensor_scalar(om[:], sg[:], -1.0, 1.0, ALU.mult, ALU.add))
                cg.link(nc.vector.reciprocal(rc[:], om[:]))
                cg.link(nc.vector.scalar_tensor_tensor(out=ex[:], in0=sg[:], scalar=1.0, in1=rc[:], op0=ALU.add, op1=ALU.mult))
                cg.link(nc.vector.tensor_reduce(col["sum"][:], ex[:], AX_X, ALU.add))
                cg.link(nc.vector.reciprocal(col["gate"][:], col["sum"][:]))
                cg.link(nc.vector.tensor_scalar(payload(c, GATE), col["gate"][:], UNSCALE, None, ALU.mult))
                dve.wait_ge(pos_done, c + 1)
                cg.link(nc.vector.tensor_tensor(pm[:], sps[:, 0, 64:64 + TPC * E].rearrange("p (t e) -> p t e", e=E), onehot[:], ALU.mult))
                cg.link(nc.vector.tensor_reduce(col["pos"][:], pm[:], AX_X, ALU.add))
                cg.link(nc.vector.tensor_scalar(col["over"][:], col["pos"][:], float(CAP), float(NOWHERE), ALU.is_ge, ALU.mult))
                cg.link(nc.vector.tensor_scalar(col["slot"][:], col["m8"][:], -float(CAP), float(E * CAP), ALU.mult, ALU.add))
                cg.link(nc.vector.tensor_tensor(col["where"][:], col["slot"][:], col["pos"][:], ALU.add))
                cg.link(nc.vector.tensor_tensor(col["slot"][:], col["where"][:], col["over"][:], ALU.add))
                nc.vector.tensor_copy(slot_ids[:, bass.ds(TPC * c, TPC)], col["slot"][:]).then_inc(slots_ready, 1)
                cg.end()

            def w1_lo(e, js):
                for j in js:
                    split_lo(wA[HI][:, 1024 * j:1024 * j + 1024], wA[LO][:, 1024 * j:1024 * j + 1024], raw[:, j, :],
                             splits_before(e, "w1") + j + 1)

            def body(b, t):
                recurrence(b)
                if t is not None:
                    t_statistics(t)
                gated(b)
                if t is not None:
                    t_lo(t)
                part_b_norms(b)
                route(b)
                place(b)

            dve.wait_ge(x_first, 16)
            t_statistics(0)
            t_lo(0)
            for n in range(RING):
                attn_weights(n)
            dve.wait_ge(small_in, 32)
            nc.vector.tensor_scalar(scale64[:], scale_in[:], WSCALE, None, ALU.mult).then_inc(small_split, 1)
            dve.wait_ge(small_split, 1)
            dve.wait_ge(x_rest, 16)
            dve.wait_ge(consts, 1)
            t_statistics(1)
            t_lo(1)
            with dve.Fori(0, NCH - 1) as c:
                body(c, c + 2)
            body(NCH - 1, None)
            w1_lo(0, range(NP))

            def e_normalise(e):
                for t in range(CT):
                    row = tile_at(CT * e + t)
                    wait(dve, nrm["e"]["lo"], CT * e)
                    nc.vector.tensor_scalar(xn[:, t, :], row[:, 0:D], row[:, MEAN:MEAN + 1], row[:, RSTD:RSTD + 1],
                                            ALU.subtract, ALU.mult).then_inc(nrm["e"]["xn"], 1)
                for t in range(CT):
                    dve.wait_ge(nrm["e"]["hi"], CT * e + t + 1)
                    nc.vector.tensor_tensor(xs[:, t, LO, :], xn[:, t, :], xs[:, t, HI, :], ALU.subtract).then_inc(nrm["e"]["lo"], 1)

            def combine(e, t):
                row = tile_at(CT * e + t)
                wait(dve, rows_out[t], 16 * e)
                nc.vector.tensor_copy(row_ids[:, t:t + 1], row[:, ID:ID + 1].bitcast(U32)).then_inc(ids_ready, 1)
                dve.wait_ge(down_done, CT * e + t + 1)
                dve.wait_ge(ids_ready, CT * e + t + 1)
                nc.vector.scalar_tensor_tensor(out=done_rows[:, t, :], in0=wps[:, t, :], scalar=row[:, GATE:GATE + 1], in1=row[:, 0:D],
                                               op0=ALU.mult, op1=ALU.add).then_inc(combined, 1)

            def expert(e, last):
                for j in range(NP):
                    dve.wait_ge(gel_ready, NP * e + j + 1)
                    g = gel[:, j % 2, :].rearrange("p (a n) -> p a n", a=2)
                    nc.vector.tensor_scalar(hid[:, HI, 2 * j:2 * j + 2, :], g, WSCALE, None, ALU.mult).then_inc(hhi_ready, 1)
                    split_lo(wB[HI][:, 1024 * j:1024 * j + 1024], wB[LO][:, 1024 * j:1024 * j + 1024], raw[:, j, :],
                             splits_before(e, "w2") + j + 1)
                    dve.wait_ge(hhi_ready, NP * e + j + 1)
                    nc.vector.scalar_tensor_tensor(out=hid[:, LO, 2 * j:2 * j + 2, :], in0=g, scalar=WSCALE, in1=hid[:, HI, 2 * j:2 * j + 2, :],
                                                   op0=ALU.mult, op1=ALU.subtract).then_inc(hlo_ready, 1)
                if not last:
                    e_normalise(e + 1)
                    w1_lo(e + 1, range(NP // 2))
                combine(e, 0)
                if not last:
                    w1_lo(e + 1, range(NP // 2, NP))
                combine(e, 1)

            dve.wait_ge(e_first, 16)
            e_normalise(0)
            dve.wait_ge(e_rest, 16)
            expert(0, False)
            with dve.Fori(1, E - 1) as e:
                expert(e, False)
            expert(E - 1, True)

        @block.tensor
        def _(pe):
            def turn(part, u, tiles, free):
                for t in range(tiles):
                    pe.wait_ge(nrm[part]["lo"], tiles * u + t + 1)
                    free(t)
                    for hl in range(2):
                        for k in range(KD):
                            last = nc.tensor.transpose(tps16[:, t % 2, hl, k, :], xs[:, t, hl, k * P:(k + 1) * P], ident[:])
                    last.then_inc(nrm[part]["turned"], 1)

            def part_t(c, after_b):
                def free(t):
                    if t >= 2:
                        pe.wait_ge(nrm["t"]["copied"], TPC * c + t - 1)
                    elif after_b is None:
                        wait(pe, nrm["t"]["copied"], TPC * c + t - 1)
                    else:
                        pe.wait_ge(nrm["b"]["copied"], TPC * after_b)
                turn("t", c, TPC, free)

            def project(c, w, m, done):
                half = c & 1
                n = 0
                for k in range(KD):
                    for a, b in PASSES:
                        last = nc.tensor.matmul(zps[:, w, :], proj[a][:, w, k, m * P:(m + 1) * P],
                                                xT[:, bass.ds(half, 1), b, k, :].rearrange("p c n -> p (c n)"),
                                                start=(n == 0), stop=(n == 3 * KD - 1))
                        n += 1
                last.then_inc(done, 1)

            def z_f(c, m):
                if first(c) and m == 0:
                    pe.wait_ge(lo_split, 2)
                if m == 0:
                    pe.wait_ge(nrm["t"]["copied"], TPC * (c + 1))
                wait(pe, f_ready, 4 * c + m)
                project(c, 0, m, zf_done)

            def z_c(c, m):
                if first(c) and m == 0:
                    pe.wait_ge(lo_split, 4)
                wait(pe, c_ready, 4 * c + m)
                project(c, 1, m, zc_done)

            def z_r(c, m):
                if first(c) and m == 0:
                    pe.wait_ge(lo_split, 6)
                wait(pe, r_ready, 4 * c + m)
                project(c, 2, m, zr_done)

            def out_projection(c):
                pe.wait_ge(hsq_ready, 4 * (c + 1))
                wait(pe, slots_ready, c)
                for t in range(TPC):
                    for m in range(KD):
                        last = nc.tensor.matmul(sps[:, 0, t:t + 1], hsq[:, m, t * P:(t + 1) * P], ones32[:], start=(m == 0), stop=(m == KD - 1))
                last.then_inc(rms_done, 1)
                pe.wait_ge(plo_ready, 4 * (c + 1))
                pe.wait_ge(lo_split, RING)
                for t in range(TPC):
                    wait(pe, x1_ready, two_before(TPC * c, t))
                    n = 0
                    for m in range(KD):
                        for a, b in PASSES:
                            last = nc.tensor.matmul(wps[:, t % 2, :], pT[a][:, m, t * P:(t + 1) * P], proj[b][:, 3, m, :],
                                                    start=(n == 0), stop=(n == 3 * KD - 1))
                            n += 1
                    last.then_inc(wo_done, 1)

            def logits(c, t):
                pe.wait_ge(nrm["b"]["copied"], TPC * c + t + 1)
                if t == 0:
                    pe.wait_ge(rms_var, c + 1)
                for k in range(KD):
                    last = nc.tensor.matmul(sps[:, 0, 32 + t * E:32 + (t + 1) * E], x1T[:, t % 2, k, :], wg_in[:, k, :],
                                            start=(k == 0), stop=(k == KD - 1))
                if t == TPC - 1:
                    last.then_inc(logits_done, 1)

            def route(c):
                t_parts = min(c + 3, NCH + 1) if isinstance(c, int) else c + 3
                for t in range(TPC):
                    pe.wait_ge(nrm["b"]["xn"], TPC * c + t + 1)
                    if t >= 2:
                        pe.wait_ge(nrm["b"]["copied"], TPC * c + t - 1)
                    else:
                        pe.wait_ge(nrm["t"]["copied"], TPC * t_parts)
                    for k in range(KD):
                        last = nc.tensor.transpose(tps32[:, t % 2, k, :], x1n[:, t, k * P:(k + 1) * P], ident32[:])
                    last.then_inc(nrm["b"]["turned"], 1)
                    if t >= 1:
                        logits(c, t - 1)
                logits(c, TPC - 1)

            def positions(c):
                pe.wait_ge(onehot_ready, c + 1)
                nc.tensor.matmul(sps[:, 0, 64:64 + TPC * E], earlier[:], onehot[:].rearrange("p t e -> p (t e)"), start=True, stop=False)
                nc.tensor.matmul(sps[:, 0, 64:64 + TPC * E], ones16[:], before[:, 0:TPC, :].rearrange("p t e -> p (t e)"),
                                 start=False, stop=True).then_inc(pos_done, 1)

            def body(a, b, t):
                if a is not None:
                    for m in range(KD - 1):
                        z_f(a, m)
                        z_c(a, m)
                        z_r(a, m)
                if b is not None:
                    out_projection(b)
                if t is not None:
                    part_t(t, b)
                if a is not None:
                    z_f(a, KD - 1)
                    z_c(a, KD - 1)
                    z_r(a, KD - 1)
                if b is not None:
                    route(b)
                    positions(b)

            pe.wait_ge(consts, 1)
            pe.wait_ge(small_in, 32)
            part_t(0, None)
            part_t(1, None)
            body(0, None, None)
            with pe.Fori(1, NCH) as c:
                body(c, c - 1, c + 1)
            body(None, NCH - 1, None)

            def turn_expert(e):
                if isinstance(e, int) and e == 0:
                    turn("e", e, CT, lambda t: None)
                else:
                    turn("e", e, CT, lambda t: pe.wait_ge(nrm["e"]["copied"], CT * e))

            def up(e, j):
                pe.wait_ge(lo_split, splits_before(e, "w1") + j + 1)
                if j == 0:
                    pe.wait_ge(nrm["e"]["copied"], CT * (e + 1))
                wait(pe, gel_ready, NP * e + (j - 1 if j < 2 else j - 2))
                for f in range(2):
                    n = 0
                    for k in range(KD):
                        for a, b in PASSES:
                            last = nc.tensor.matmul(zps[:, j % 3, f * CAP:(f + 1) * CAP], w1s[a][:, j, k, f * P:(f + 1) * P], xTe[:, b, k, :],
                                                    start=(n == 0), stop=(n == 3 * KD - 1))
                            n += 1
                last.then_inc(up_done, 1)

            def down(e, t, turns):
                wait(pe, combined, CT * (e - 1) + t + 1)
                n = 0
                for j in range(NP):
                    if t == 0:
                        pe.wait_ge(lo_split, splits_before(e, "w2") + j + 1)
                        pe.wait_ge(hlo_ready, NP * e + j + 1)
                    for f in range(2):
                        for a, b in PASSES:
                            last = nc.tensor.matmul(wps[:, t, :], hid[:, a, 2 * j + f, t * P:(t + 1) * P], w2s[b][:, j, f, :],
                                                    start=(n == 0), stop=(n == 6 * NP - 1))
                            n += 1
                last.then_inc(down_done, 1)

            def expert(e, last):
                for j in range(NP):
                    up(e, j)
                down(e, 0, False)
                if not last:
                    turn_expert(e + 1)
                down(e, 1, False)

            turn_expert(0)
            expert(0, False)
            with pe.Fori(1, E - 1) as e:
                expert(e, False)
            expert(E - 1, True)


_INS = ["L0_attn_x", "L0_attn_Wr", "L0_attn_Wf", "L0_attn_Wc", "L0_attn_Wo", "L0_attn_ln_scale", "L0_ffn_w_gate", "L0_ffn_w1", "L0_ffn_w2"]
_OUTS = [((2, 1024, 512), "float32")]


def kernel(**inputs):
    import numpy as _np
    import concourse.bacc as _bacc
    from concourse import mybir as _mybir
    from concourse.bass_utils import run_bass_kernel_spmd as _run

    nc = _bacc.Bacc("TRN2", target_bir_lowering=False, num_devices=1)
    arrays, args = {}, []
    for name in _INS:
        a = _np.ascontiguousarray(inputs[name])
        arrays[f"in_{name}_dram"] = a
        args.append(nc.dram_tensor(f"in_{name}_dram", a.shape, _mybir.dt.from_np(a.dtype), kind="ExternalInput").ap())
    for i, (shape, dtype) in enumerate(_OUTS):
        dt = _mybir.dt.from_np(_np.dtype(dtype))
        args.append(nc.dram_tensor(f"out_{i}_dram", shape, dt, kind="ExternalOutput").ap())
    recurrent_block_with_experts(nc, *args)
    r = _run(nc, [arrays], core_ids=[0])
    return r.results[0]["out_0_dram"]
```

```python
from contextlib import ExitStack

import concourse.bass as bass
from concourse import mybir

P = 128
F32 = mybir.dt.float32
F16 = mybir.dt.float16
U32 = mybir.dt.uint32
ALU = mybir.AluOpType
ACT = mybir.ActivationFunctionType
AX_X = mybir.AxisListType.X

EPS = 1e-5
WSCALE = 64.0
UNSCALE = WSCALE**-2
HI, LO = 0, 1
PASSES = ((HI, HI), (HI, LO), (LO, HI))


class Chain:

    def __init__(self, sem, engine, per_unit):
        self.sem, self.engine, self.per_unit, self.done = sem, engine, per_unit, 0

    def start(self, unit):
        self.base, self.done = unit * self.per_unit, 0

    def step(self, instruction):
        instruction.then_inc(self.sem, 1)
        self.done += 1
        return self.base + self.done

    def after(self, value):
        self.engine.wait_ge(self.sem, value)

    def link(self, instruction):
        self.after(self.step(instruction))

    def end(self):
        assert self.done == self.per_unit, (self.sem, self.done)


def recurrent_block_with_experts(nc, x, Wr, Wf, Wc, Wo, ln_scale, w_gate, w1, w2, out):
    B, S, D = x.shape
    E, _, F = w1.shape
    TOK = B * S
    CAP = TOK // E
    CH = 512
    NCH = TOK // CH
    TPC = CH // P
    NT = TOK // P
    KD = D // P
    NP = F // 256
    CT = CAP // P
    RING = 8
    AW = 4
    XW = D + 4
    MEAN, RSTD, GATE, ID = D, D + 1, D + 2, D + 3
    NOWHERE = 1 << 20
    TREE = 3 * 9 + 3 * 10 - 1
    assert AW * KD * D == RING * 1024 and NP == RING and KD * 256 == 1024 and S % CH == 0 and CT == 2
    CHUNKS_PER_SEQ = S // CH
    assert CHUNKS_PER_SEQ == 2

    x_rows = x.rearrange("b s d -> (b s) d")
    out_rows = out.rearrange("b s d -> (b s) d")
    x_tiles = x_rows.rearrange("(t p) d -> p t d", p=P)
    out_tiles = out_rows.rearrange("(t p) d -> p t d", p=P)
    table = nc.dram_tensor("expert_rows", (E * CAP, XW), F32, kind="Internal").ap()
    table_tiles = table.rearrange("(t p) d -> p t d", p=P)
    w1_chunks = w1.rearrange("e (k p) (j n) -> e j p k n", p=P, j=NP)
    w2_chunks = w2.rearrange("e (j a p) n -> e j p a n", p=P, j=NP)

    with ExitStack() as ctx:
        def sb(name, shape, dt=F32):
            return ctx.enter_context(nc.sbuf_tensor(name, shape, dt))

        def sem(name):
            return ctx.enter_context(nc.semaphore(name))

        rows = sb("rows", [P, NT, XW])
        raw = sb("raw", [P, RING, 1024])
        wB = [sb("wB_hi", [P, RING * 1024], F16), sb("wB_lo", [P, RING * 1024], F16)]
        wA = [sb("wA_hi", [P, RING * 1024], F16), sb("wA_lo", [P, RING * 1024], F16)]
        proj = [w[:].rearrange("p (w k n) -> p w k n", w=AW, k=KD) for w in wB]
        w2s = [w[:].rearrange("p (j a n) -> p j a n", j=NP, a=2) for w in wB]
        w1s = [w[:].rearrange("p (j k n) -> p j k n", j=NP, k=KD) for w in wA]
        xT = sb("xT", [P, 2, 2, KD, CH], F16)
        xTe = xT[:, 0].rearrange("p h k n -> p (h k n)")[:, 0:2 * KD * CAP].rearrange("p (h k n) -> p h k n", h=2, k=KD)
        f_all = wA[HI][:].bitcast(F32).rearrange("p (c m n) -> p c m n", c=2, m=KD)
        r_all = wA[LO][:].bitcast(F32).rearrange("p (c m n) -> p c m n", c=2, m=KD)
        state = sb("state", [P, 2, KD, 1 + CH])
        hid = state[:].rearrange("p c m n -> p (c m n)").bitcast(F16)[:, 0:2 * F // P * CAP].rearrange("p (h f n) -> p h f n", h=2, n=CAP)
        tmp = sb("tmp", [P, KD, CH // 2])
        gel = tmp[:].rearrange("p m n -> p (m n)").rearrange("p (b n) -> p b n", b=2)
        hsq = sb("hsq", [P, KD, CH])
        pT = [sb("pT_hi", [P, KD, CH], F16), sb("pT_lo", [P, KD, CH], F16)]
        done_rows = hsq[:, 0:2, :]
        xn = sb("xn", [P, 2, D])
        xs = sb("xs", [P, TPC, 2, D], F16)
        x1n = sb("x1n", [P, TPC, D])
        x1T = sb("x1T", [P, 2, KD, P])
        fill = x1T[:].rearrange("p b k n -> p (b k n)")[:, 0:XW]
        ident = sb("ident", [P, P], F16)
        ident32 = sb("ident32", [P, P])
        earlier = sb("earlier", [P, P], F16)
        ones16 = sb("ones16", [P, P], F16)
        ones32 = sb("ones32", [P, 1])
        neg_half = sb("neg_half", [P, TPC])
        rank = sb("rank", [P, TPC, E])
        scale64 = sb("scale64", [P, KD])
        scale_in = sb("scale_in", [P, KD])
        wg_in = sb("wg_in", [P, KD, E])
        keep = sb("keep", [P, NCH])
        width = {"t": NT, "b": TPC, "r": TPC}
        st = {n: sb(f"st_{n}", [P, TPC, 6]) for n in "tb"}
        mv = sb("mv", [P, TPC, 2])
        rs = {n: sb(f"rs_{n}", [P, width[n]]) for n in "tbr"}
        shift = {n: sb(f"shift_{n}", [P, width[n]]) for n in "tb"}
        small = {n: sb(f"sm_{n}", [P, TPC, E]) for n in ("lg", "d", "sg", "om", "rc", "eq")}
        small["ex"], small["pm"] = small["om"], small["lg"]
        col = {n: sb(f"col_{n}", [P, TPC]) for n in ("max", "ms", "sum", "gate", "m8", "pos", "slot", "over", "where")}
        onehot = sb("onehot", [P, TPC, E], F16)
        before = sb("before", [P, TPC + 1, E], F16)
        slot_ids = sb("slot_ids", [P, NT], U32)
        row_ids = sb("row_ids", [P, CT], U32)

        def bank(name, n, dt=F32):
            return ctx.enter_context(nc.psum_tensor(name, [P, n, 2048 // (4 if dt == F32 else 2)], dt))

        zps = bank("zps", 3)
        sps = bank("sps", 1)
        tps = bank("tps", 2, F16)
        wps = bank("wps", 2)
        tps16 = tps[:].rearrange("p b (h k n) -> p b h k n", h=2, k=KD)
        tps32 = tps[:].bitcast(F32).rearrange("p b (k n) -> p b k n", k=KD)

        x_first, x_rest, small_in = sem("x_first"), sem("x_rest"), sem("small_in")
        raw_in = [sem(f"raw_in{i}") for i in range(RING)]
        hi_split, lo_split = sem("hi_split"), sem("lo_split")
        small_split = sem("small_split")
        consts, setup = sem("consts"), sem("setup")
        table_clear, scattered, base_out = sem("table_clear"), sem("scattered"), sem("base_out")
        nrm = {p: {n: sem(f"{p}_{n}") for n in ("var", "rstd", "xn", "hi", "lo", "turned", "copied")} for p in "tbe"}
        chain_s, chain_n, chain_g = sem("chain_s"), sem("chain_n"), sem("chain_g")
        zf_done, zc_done, zr_done = sem("zf_done"), sem("zc_done"), sem("zr_done")
        tanh_ready, f_ready, c_ready, r_ready = sem("tanh_ready"), sem("f_ready"), sem("c_ready"), sem("r_ready")
        tree_step, states_ready, hsq_ready, phi_ready, p_ready, plo_ready = (
            sem(n) for n in ("tree_step", "states_ready", "hsq_ready", "phi_ready", "p_ready", "plo_ready"))
        rms_done, rms_var, rms_rstd, wo_done, x1_ready = (sem(n) for n in ("rms_done", "rms_var", "rms_rstd", "wo_done", "x1_ready"))
        logits_done, diff_ready, sig_ready, onehot_ready, pos_done, slots_ready = (
            sem(n) for n in ("logits_done", "diff_ready", "sig_ready", "onehot_ready", "pos_done", "slots_ready"))
        e_first, e_rest = sem("e_first"), sem("e_rest")
        up_done, gel_ready, hhi_ready, hlo_ready, down_done = (sem(n) for n in ("up_done", "gel_ready", "hhi_ready", "hlo_ready", "down_done"))
        ids_ready, combined, rows_out = sem("ids_ready"), sem("combined"), [sem(f"rows_out{t}") for t in range(CT)]

        block = ctx.enter_context(nc.Block())

        def wait(eng, s, value):
            if not isinstance(value, int) or value > 0:
                eng.wait_ge(s, value)

        def two_before(count, t):
            return count + max(t - 1, 0)

        def xs_slot(part, t):
            return t if part == "b" else t % 2

        def sums_bank(c):
            return sps[:, 0, :] if c < NCH - 1 else zps[:, 0, :]

        def first(unit):
            return isinstance(unit, int) and unit == 0

        def tile_at(t):
            return rows[:, bass.ds(t, 1), :].rearrange("p a d -> p (a d)")

        def splits_before(e, matrix):
            return RING * (1 + 2 * e + (matrix == "w2"))

        def raw_wait(eng, e, matrix, j):
            eng.wait_ge(raw_in[j], 16 * (splits_before(e, matrix) // RING + 1) if isinstance(e, int)
                        else 32 * e + (48 if matrix == "w2" else 32))

        @block.sync
        def _(sp):
            sp.dma_start(rows[:, 0:TPC, 0:D], x_tiles[:, 0:TPC, :]).then_inc(x_first, 16)
            for i, w in enumerate((Wf, Wc, Wr, Wo)):
                w_in = w.rearrange("(k p) n -> p k n", p=P)
                for half in range(2):
                    sp.dma_start(raw[:, 2 * i + half, :].rearrange("p (k n) -> p k n", k=2),
                                 w_in[:, 2 * half:2 * half + 2, :]).then_inc(raw_in[2 * i + half], 16)
                if i == 0:
                    with nc.allow_non_contiguous_dma(reason="2 KB in all"):
                        sp.dma_start(scale_in[:], ln_scale.rearrange("(k p) -> p k", p=P)).then_inc(small_in, 16)
                    sp.dma_start(wg_in[:], w_gate.rearrange("(k p) e -> p k e", p=P)).then_inc(small_in, 16)
                if i == 2:
                    sp.dma_start(rows[:, TPC:NT, 0:D], x_tiles[:, TPC:NT, :]).then_inc(x_rest, 16)
            sp.wait_ge(consts, 1)
            for t in range(NT):
                sp.dma_start(table_tiles[:, t, :], fill).then_inc(table_clear, 16)

            def load(e, matrix):
                for j in range(NP):
                    sp.wait_ge(lo_split, splits_before(e, matrix) - RING + j + 1)
                    if matrix == "w1":
                        src = w1_chunks[bass.ds(e, 1), j].rearrange("e p k n -> p (e k) n")
                        dst = raw[:, j, :].rearrange("p (k n) -> p k n", k=KD)
                    else:
                        src = w2_chunks[bass.ds(e, 1), j].rearrange("e p a n -> p (e a) n")
                        dst = raw[:, j, :].rearrange("p (a n) -> p a n", a=2)
                    sp.dma_start(dst, src).then_inc(raw_in[j], 16)

            load(0, "w1")
            load(0, "w2")
            sp.wait_ge(scattered, 16 * NT)
            sp.wait_ge(base_out, 16 * NCH)
            sp.dma_start(rows[:, 0:CT, :], table_tiles[:, 0:CT, :]).then_inc(e_first, 16)
            sp.dma_start(rows[:, CT:NT, :], table_tiles[:, CT:NT, :]).then_inc(e_rest, 16)
            with sp.Fori(1, E) as e:
                load(e, "w1")
                load(e, "w2")

        @block.gpsimd
        def _(pool):
            steps = [0]

            def made(instruction):
                steps[0] += 1
                instruction.then_inc(setup, 1)
                return steps[0]

            made(nc.gpsimd.memset(fill, 0.0))
            made(nc.gpsimd.memset(ident[:], 1.0))
            made(nc.gpsimd.memset(earlier[:], 1.0))
            made(nc.gpsimd.memset(ones16[:], 1.0))
            made(nc.gpsimd.memset(ones32[:], 1.0))
            made(nc.gpsimd.memset(neg_half[:], -0.5))
            made(nc.gpsimd.memset(state[:, 0, :, 0:1], 0.0))
            made(nc.gpsimd.memset(ident32[:], 1.0))
            made(nc.gpsimd.memset(keep[:], 1.0))
            made(nc.gpsimd.memset(before[:], 0.0))
            pool.wait_ge(setup, steps[0])
            made(nc.gpsimd.iota(fill[:, ID:ID + 1].bitcast(U32), pattern=[[0, 1]], base=NOWHERE, channel_multiplier=0))
            for e in range(E):
                made(nc.gpsimd.memset(rank[:, :, e], float(E - e)))
            for c in range(0, NCH, CHUNKS_PER_SEQ):
                made(nc.gpsimd.memset(keep[:, c:c + 1], 0.0))
            made(nc.gpsimd.affine_select(out=ident[:], in_=ident[:], compare_op=ALU.is_equal, fill=0.0,
                                         base=0, pattern=[[-1, P]], channel_multiplier=1))
            made(nc.gpsimd.affine_select(out=ident32[:], in_=ident32[:], compare_op=ALU.is_equal, fill=0.0,
                                         base=0, pattern=[[-1, P]], channel_multiplier=1))
            made(nc.gpsimd.affine_select(out=earlier[:], in_=earlier[:], compare_op=ALU.is_gt, fill=0.0,
                                         base=0, pattern=[[1, P]], channel_multiplier=-1))
            pool.wait_ge(setup, steps[0])
            for t in range(NT):
                made(nc.gpsimd.iota(rows[:, t, ID:ID + 1].bitcast(U32), pattern=[[0, 1]], base=t * P, channel_multiplier=1))
            pool.wait_ge(setup, steps[0])
            nc.gpsimd.memset(slot_ids[:], 0).then_inc(consts, 1)

            def power(part, count, tiles):
                pool.wait_ge(nrm[part]["var"], count)
                made(nc.gpsimd.tensor_tensor(rs[part][:, tiles], rs[part][:, tiles], neg_half[:, 0:tiles.stop - tiles.start], ALU.pow))
                pool.wait_ge(setup, steps[0])
                nc.gpsimd.tensor_tensor(shift[part][:, tiles], shift[part][:, tiles], rs[part][:, tiles], ALU.mult).then_inc(nrm[part]["rstd"], 1)

            def t_lo(c):
                for t in range(TPC):
                    pool.wait_ge(nrm["t"]["hi"], TPC * c + t + 1)
                    nc.gpsimd.tensor_tensor(xs[:, t, LO, :], xn[:, t % 2, :], xs[:, t, HI, :], ALU.subtract).then_inc(nrm["t"]["lo"], 1)

            def part_b_norms(c, between=None):
                pool.wait_ge(rms_var, c + 1)
                nc.gpsimd.tensor_tensor(rs["r"][:], rs["r"][:], neg_half[:], ALU.pow).then_inc(rms_rstd, 1)
                if between is not None:
                    between()
                for t in range(TPC):
                    power("b", TPC * c + t + 1, slice(t, t + 1))
                pool.wait_ge(x1_ready, TPC * (c + 1))
                pool.dma_start(out_tiles[:, TPC * c:TPC * c + TPC, :], rows[:, TPC * c:TPC * c + TPC, 0:D]).then_inc(base_out, 16)

            def scatter(c):
                pool.wait_ge(slots_ready, c + 1)
                if c == 0:
                    pool.wait_ge(table_clear, 16 * NT)
                for t in range(TPC * c, TPC * c + TPC):
                    pool.indirect_dma_start(
                        out=table, out_offset=bass.IndirectOffsetOnAxis(ap=slot_ids[:, t:t + 1], axis=0),
                        in_=rows[:, t, :], in_offset=None, bounds_check=E * CAP - 1, oob_is_err=False).then_inc(scattered, 16)

            def w1_lo(j):
                pool.wait_ge(hi_split, splits_before(0, "w1") + j + 1)
                made(nc.gpsimd.tensor_scalar(raw[:, j, :], raw[:, j, :], WSCALE, None, ALU.mult))
                pool.wait_ge(setup, steps[0])
                nc.gpsimd.tensor_tensor(wA[LO][:, 1024 * j:1024 * j + 1024], raw[:, j, :], wA[HI][:, 1024 * j:1024 * j + 1024],
                                        ALU.subtract).then_inc(lo_split, 1)

            for c in range(NCH):
                power("t", c + 1, slice(TPC * c, TPC * c + TPC))
                t_lo(c)
            for c in range(NCH - 2):
                part_b_norms(c)
                scatter(c)
            part_b_norms(NCH - 2, lambda: w1_lo(0))
            for j in range(1, NP // 2):
                w1_lo(j)
            scatter(NCH - 2)
            part_b_norms(NCH - 1)
            scatter(NCH - 1)

            for e in range(E):
                for t in range(CT):
                    pool.wait_ge(combined, CT * e + t + 1)
                    pool.indirect_dma_start(
                        out=out_rows, out_offset=bass.IndirectOffsetOnAxis(ap=row_ids[:, t:t + 1], axis=0),
                        in_=done_rows[:, t, :], in_offset=None, bounds_check=TOK - 1, oob_is_err=False).then_inc(rows_out[t], 16)
            for t in range(CT):
                pool.wait_ge(rows_out[t], 16 * E)

        @block.scalar
        def _(act):
            def attn_weights(n):
                act.wait_ge(raw_in[n], 16)
                nc.scalar.activation(wB[HI][:, 1024 * n:1024 * n + 1024], raw[:, n, :], ACT.Copy, scale=WSCALE).then_inc(hi_split, 1)

            def normal(u, src):
                for t in range(TPC):
                    if t == 0:
                        act.wait_ge(nrm["t"]["rstd"], u + 1)
                        wait(act, nrm["t"]["turned"], TPC * u)
                    wait(act, nrm["t"]["lo"], two_before(TPC * u, t))
                    for dst in (xn[:, t % 2, :], xs[:, t, HI, :]):
                        last = nc.scalar.activation(dst, src(t), ACT.Identity, scale=rs["t"][:, bass.ds(TPC * u + t, 1)],
                                                    bias=shift["t"][:, bass.ds(TPC * u + t, 1)])
                    last.then_inc(nrm["t"]["hi"], 1)

            def normal_x1(c, *tiles):
                for t in tiles:
                    act.wait_ge(nrm["b"]["rstd"], TPC * c + t + 1)
                    wait(act, nrm["b"]["turned"], TPC * (c - 1) + t + 1)
                    nc.scalar.activation(x1n[:, t, :], tile_at(TPC * c + t)[:, 0:D], ACT.Identity, scale=rs["b"][:, t:t + 1],
                                         bias=shift["b"][:, t:t + 1]).then_inc(nrm["b"]["xn"], 1)

            def copy_turned(part, u, tiles, dst, src, some=None):
                for t in some or range(tiles):
                    act.wait_ge(nrm[part]["turned"], tiles * u + t + 1)
                    nc.scalar.activation(dst(t), src[:, t % 2], ACT.Copy).then_inc(nrm[part]["copied"], 1)

            def t_copies(c):
                wait(act, zr_done, 4 * (c - 1))
                copy_turned("t", c, TPC, lambda t: xT[:, bass.ds(c & 1, 1), :, :, t * P:(t + 1) * P].rearrange("p c h k n -> p (c h) k n"), tps16)

            def of_chunk(a, c, m):
                return a[:, bass.ds(c & 1, 1), m, :].rearrange("p c n -> p (c n)")

            def gates(c, m):
                act.wait_ge(zf_done, 4 * c + m + 1)
                if m == 0:
                    wait(act, p_ready, 4 * (c - 1))
                    wait(act, plo_ready, 4 * (c - 1))
                nc.scalar.activation(zps[:, 0, :], zps[:, 0, :], ACT.Tanh, scale=UNSCALE / 2).then_inc(tanh_ready, 1)
                act.wait_ge(zc_done, 4 * c + m + 1)
                nc.scalar.activation(of_chunk(state, c, m)[:, 1:1 + CH], zps[:, 1, :], ACT.Silu, scale=UNSCALE).then_inc(c_ready, 1)
                act.wait_ge(tanh_ready, 4 * c + m + 1)
                nc.scalar.activation(of_chunk(f_all, c, m), zps[:, 0, :], ACT.Copy, scale=0.5, bias=0.5).then_inc(f_ready, 1)
                act.wait_ge(zr_done, 4 * c + m + 1)
                nc.scalar.activation(of_chunk(r_all, c, m), zps[:, 2, :], ACT.Silu, scale=UNSCALE).then_inc(r_ready, 1)

            def squares(c):
                act.wait_ge(states_ready, c + 1)
                wait(act, rms_done, c)
                for m in range(KD):
                    nc.scalar.activation(hsq[:, m, :], of_chunk(state, c, m)[:, 1:1 + CH], ACT.Square).then_inc(hsq_ready, 1)

            def p_hi(c):
                for m in range(KD):
                    act.wait_ge(p_ready, 4 * c + m + 1)
                    if m == 0:
                        wait(act, wo_done, TPC * c)
                    nc.scalar.activation(pT[HI][:, m, :], of_chunk(r_all, c, m), ACT.Copy).then_inc(phi_ready, 1)

            def tanh_of_diff(c):
                act.wait_ge(diff_ready, c + 1)
                nc.scalar.activation(small["sg"][:], small["d"][:], ACT.Tanh, scale=0.5 / WSCALE).then_inc(sig_ready, 1)

            def x_tile(c):
                return lambda t: tile_at(TPC * c + t)[:, 0:D]

            def b_copies(c, *some):
                copy_turned("b", c, TPC, lambda t: x1T[:, t % 2], tps32, some)

            def last_part_b(c):
                for t in range(TPC):
                    normal_x1(c, t)
                    if t >= 1:
                        b_copies(c, t - 1)
                b_copies(c, TPC - 1)
                tanh_of_diff(c)

            def w1_hi(e, js=range(NP)):
                for j in js:
                    raw_wait(act, e, "w1", j)
                    if j == 0:
                        wait(act, up_done, NP * e)
                    if first(e) and j in (0, NP // 2):
                        act.wait_ge(plo_ready, KD * (NCH - 1 if j == 0 else NCH))
                    nc.scalar.activation(wA[HI][:, 1024 * j:1024 * j + 1024], raw[:, j, :], ACT.Copy, scale=WSCALE).then_inc(hi_split, 1)

            def expert_hi(e):
                for t in range(CT):
                    act.wait_ge(nrm["e"]["xn"], CT * e + t + 1)
                    if t == 0:
                        act.wait_ge(nrm["t"]["turned"], NT)
                        wait(act, nrm["e"]["turned"], CT * e)
                    nc.scalar.activation(xs[:, t, HI, :], xn[:, t, :], ACT.Copy).then_inc(nrm["e"]["hi"], 1)

            normal(0, x_tile(0))
            for n in range(6):
                attn_weights(n)
            t_copies(0)
            attn_weights(6)
            attn_weights(7)
            gates(0, 0)
            normal(1, x_tile(1))
            gates(0, 1)
            t_copies(1)
            gates(0, 2)
            gates(0, 3)
            gates(1, 0)
            normal(2, x_tile(2))
            gates(1, 1)
            t_copies(2)
            gates(1, 2)
            squares(0)
            p_hi(0)
            gates(1, 3)
            act.wait_ge(table_clear, 16 * NT)
            for c in range(2, NCH):
                if c + 1 < NCH:
                    normal(c + 1, x_tile(c + 1))
                    t_copies(c + 1)
                normal_x1(c - 2, 0, 1)
                b_copies(c - 2, 0, 1)
                normal_x1(c - 2, 2, 3)
                gates(c, 0)
                b_copies(c - 2, 2, 3)
                gates(c, 1)
                tanh_of_diff(c - 2)
                squares(c - 1)
                gates(c, 2)
                p_hi(c - 1)
                gates(c, 3)
            w1_hi(0, range(NP // 2))
            last_part_b(NCH - 2)
            squares(NCH - 1)
            p_hi(NCH - 1)
            w1_hi(0, range(NP // 2, NP))
            last_part_b(NCH - 1)

            def e_copies(e):
                copy_turned("e", e, CT, lambda t: xTe[:, :, :, t * P:(t + 1) * P], tps16)

            def expert(e, last):
                for j in range(NP):
                    act.wait_ge(up_done, NP * e + j + 1)
                    wait(act, hlo_ready, NP * e + j - 1)
                    nc.scalar.activation(gel[:, j % 2, :], zps[:, j % 3, :], ACT.Gelu_apprx_tanh, scale=UNSCALE).then_inc(gel_ready, 1)
                    raw_wait(act, e, "w2", j)
                    if j == 0:
                        wait(act, down_done, CT * e)
                        act.wait_ge(wo_done, NT)
                    nc.scalar.activation(wB[HI][:, 1024 * j:1024 * j + 1024], raw[:, j, :], ACT.Copy, scale=WSCALE).then_inc(hi_split, 1)
                if last:
                    return
                expert_hi(e + 1)
                act.wait_ge(up_done, NP * (e + 1))
                e_copies(e + 1)
                w1_hi(e + 1)

            expert_hi(0)
            e_copies(0)
            expert(0, False)
            with act.Fori(1, E - 1) as e:
                expert(e, False)
            expert(E - 1, True)

        @block.vector
        def _(dve):
            cs = Chain(chain_s, dve, 2)
            cn = Chain(chain_n, dve, 2)
            cg = Chain(chain_g, dve, 21)

            def split_lo(hi, lo, src, count):
                dve.wait_ge(hi_split, count)
                nc.vector.scalar_tensor_tensor(out=lo, in0=src, scalar=WSCALE, in1=hi, op0=ALU.mult, op1=ALU.subtract).then_inc(lo_split, 1)

            def attn_weights(n):
                split_lo(wB[HI][:, 1024 * n:1024 * n + 1024], wB[LO][:, 1024 * n:1024 * n + 1024], raw[:, n, :], n + 1)

            def statistics(part, first_tile, count, source, moments):
                tiles = slice(first_tile, first_tile + count)
                for t in range(count):
                    nc.vector.bn_stats(st[part][:, t, :], source(t))
                nc.vector.drain()
                for t in range(count):
                    nc.vector.bn_aggr(moments[:, t, :], st[part][:, t, :])
                nc.vector.drain()
                nc.vector.tensor_scalar(shift[part][:, tiles], moments[:, :, 0], -1.0, None, ALU.mult)
                nc.vector.tensor_scalar(rs[part][:, tiles], moments[:, :, 1], EPS, UNSCALE, ALU.add, ALU.mult).then_inc(nrm[part]["var"], 1)

            def t_statistics(c):
                statistics("t", TPC * c, TPC, lambda t: rows[:, TPC * c + t, 0:D], mv)

            tree = {"steps": 0}

            def link(c, instruction):
                tree["steps"] += 1
                instruction.then_inc(tree_step, 1)
                dve.wait_ge(tree_step, TREE * c + tree["steps"])

            def of_parity(a, c):
                return a[:, bass.ds(c & 1, 1)].rearrange("p c m n -> p (c m) n")

            def scan_up(c, after={}):
                f_c, s_c = of_parity(f_all, c), of_parity(state, c)
                tree["steps"] = 0
                cs.start(c)
                dve.wait_ge(f_ready, 4 * (c + 1))
                dve.wait_ge(c_ready, 4 * (c + 1))
                cs.link(nc.vector.tensor_tensor(f_c[:, :, 0:1], f_c[:, :, 0:1], keep[:, bass.ds(c, 1)].unsqueeze(1).to_broadcast([P, KD, 1]), ALU.mult))
                g = 2
                while g <= CH:
                    blocks = s_c[:, :, 1:1 + CH].rearrange("p m (i g) -> p m i g", g=g)
                    f_blocks = f_c.rearrange("p m (i g) -> p m i g", g=g)
                    c_left, c_right = blocks[:, :, :, g // 2 - 1], blocks[:, :, :, g - 1]
                    f_left, f_right = f_blocks[:, :, :, g // 2 - 1], f_blocks[:, :, :, g - 1]
                    t_g = tmp[:, :, 0:CH // g]
                    link(c, nc.vector.tensor_tensor(t_g, c_left, c_right, ALU.subtract))
                    link(c, nc.vector.tensor_tensor(t_g, t_g, f_right, ALU.mult))
                    nc.vector.tensor_tensor(f_right, f_right, f_left, ALU.mult)
                    link(c, nc.vector.tensor_tensor(c_right, c_right, t_g, ALU.add))
                    if g in after:
                        after[g]()
                    g *= 2

            def scan_down(c, before_level={}):
                f_c, s_c = of_parity(f_all, c), of_parity(state, c)
                g = 2 * CH
                while g >= 2:
                    if g in before_level:
                        before_level[g]()
                    if g > CH:
                        c_here, f_here, h_before = s_c[:, :, CH:CH + 1], f_c[:, :, CH - 1:CH], s_c[:, :, 0:1]
                    else:
                        c_here = s_c[:, :, 1:1 + CH].rearrange("p m (i g) -> p m i g", g=g)[:, :, :, g // 2 - 1]
                        f_here = f_c.rearrange("p m (i g) -> p m i g", g=g)[:, :, :, g // 2 - 1]
                        h_before = s_c[:, :, 0:CH].rearrange("p m (i g) -> p m i g", g=g)[:, :, :, 0]
                    t_g = tmp[:, :, 0:max(CH // g, 1)]
                    link(c, nc.vector.tensor_tensor(t_g, h_before, c_here, ALU.subtract))
                    link(c, nc.vector.tensor_tensor(t_g, t_g, f_here, ALU.mult))
                    last = nc.vector.tensor_tensor(c_here, c_here, t_g, ALU.add)
                    if g > 2:
                        link(c, last)
                    else:
                        last.then_inc(states_ready, 1)
                    g //= 2
                assert tree["steps"] == TREE
                dve.wait_ge(states_ready, c + 1)
                cs.link(nc.vector.tensor_copy(of_parity(state, c + 1)[:, :, 0:1], s_c[:, :, CH:CH + 1]))

            def gated(c):
                for m in range(KD + 1):
                    if m < KD:
                        if m == 0:
                            dve.wait_ge(r_ready, 4 * (c + 1))
                        r = r_all[:, bass.ds(c & 1, 1), m, :].rearrange("p c n -> p (c n)")
                        h = state[:, bass.ds(c & 1, 1), m, 1:1 + CH].rearrange("p c n -> p (c n)")
                        nc.vector.scalar_tensor_tensor(out=r, in0=h, scalar=scale64[:, m:m + 1], in1=r, op0=ALU.mult, op1=ALU.mult).then_inc(p_ready, 1)
                    if m >= 1:
                        dve.wait_ge(phi_ready, 4 * c + m)
                        r = r_all[:, bass.ds(c & 1, 1), m - 1, :].rearrange("p c n -> p (c n)")
                        nc.vector.tensor_tensor(pT[LO][:, m - 1, :], r, pT[HI][:, m - 1, :], ALU.subtract).then_inc(plo_ready, 1)

            def rms_scale(c):
                dve.wait_ge(rms_done, c + 1)
                cn.start(c)
                cn.link(nc.vector.tensor_scalar(col["ms"][:], sums_bank(c)[:, 0:TPC], 1.0 / D, EPS, ALU.mult, ALU.add))
                nc.vector.tensor_scalar(rs["r"][:], col["ms"][:], UNSCALE**-2, None, ALU.mult).then_inc(rms_var, 1)

            def x1_tile(c, t):
                row = rows[:, TPC * c + t, :]
                dve.wait_ge(rms_rstd, c + 1)
                dve.wait_ge(wo_done, TPC * c + t + 1)
                nc.vector.scalar_tensor_tensor(out=row[:, 0:D], in0=wps[:, t % 2, :], scalar=rs["r"][:, t:t + 1], in1=row[:, 0:D],
                                               op0=ALU.mult, op1=ALU.add).then_inc(x1_ready, 1)
                dve.wait_ge(x1_ready, TPC * c + t + 1)
                wait(dve, nrm["b"]["xn"], TPC * (c - 1) + t + 1)
                statistics("b", t, 1, lambda i: row[:, 0:D], row[:, MEAN:MEAN + 2].unsqueeze(1))

            def rstd_payload(c):
                dve.wait_ge(nrm["b"]["rstd"], TPC * (c + 1))
                cn.link(nc.vector.tensor_copy(payload(c, RSTD), rs["b"][:]))
                cn.end()

            def payload(c, what):
                return rows[:, bass.ds(TPC * c, TPC), what]

            def each(a):
                return a[:].unsqueeze(2).to_broadcast([P, TPC, E])

            def route(c):
                d, eq = small["d"], small["eq"]
                cg.start(c)
                dve.wait_ge(logits_done, c + 1)
                cg.link(nc.vector.tensor_copy(small["lg"][:], sps[:, 0, 32:32 + TPC * E].rearrange("p (t e) -> p t e", e=E)))
                cg.link(nc.vector.tensor_reduce(col["max"][:], small["lg"][:], AX_X, ALU.max))
                nc.vector.tensor_tensor(d[:], small["lg"][:], each(col["max"]), ALU.subtract).then_inc(diff_ready, 1)
                dve.wait_ge(diff_ready, c + 1)
                cg.link(nc.vector.scalar_tensor_tensor(out=eq[:], in0=d[:], scalar=0.0, in1=rank[:], op0=ALU.is_ge, op1=ALU.mult))
                cg.link(nc.vector.tensor_reduce(col["m8"][:], eq[:], AX_X, ALU.max))
                cg.link(nc.vector.tensor_tensor(onehot[:], rank[:], each(col["m8"]), ALU.is_equal))
                cg.link(nc.vector.tensor_copy(before[:, 0, :], before[:, TPC, :]))
                for t in range(TPC - 1):
                    cg.link(nc.vector.tensor_tensor(before[:, t + 1, :], before[:, t, :], onehot[:, t, :], ALU.add))
                nc.vector.tensor_tensor(before[:, TPC, :], before[:, TPC - 1, :], onehot[:, TPC - 1, :], ALU.add).then_inc(onehot_ready, 1)

            def place(c):
                sg, om, rc, ex, pm = (small[n] for n in ("sg", "om", "rc", "ex", "pm"))
                dve.wait_ge(sig_ready, c + 1)
                cg.link(nc.vector.tensor_scalar(om[:], sg[:], -1.0, 1.0, ALU.mult, ALU.add))
                cg.link(nc.vector.reciprocal(rc[:], om[:]))
                cg.link(nc.vector.scalar_tensor_tensor(out=ex[:], in0=sg[:], scalar=1.0, in1=rc[:], op0=ALU.add, op1=ALU.mult))
                cg.link(nc.vector.tensor_reduce(col["sum"][:], ex[:], AX_X, ALU.add))
                cg.link(nc.vector.reciprocal(col["gate"][:], col["sum"][:]))
                cg.link(nc.vector.tensor_scalar(payload(c, GATE), col["gate"][:], UNSCALE, None, ALU.mult))
                dve.wait_ge(pos_done, c + 1)
                cg.link(nc.vector.tensor_tensor(pm[:], sps[:, 0, 64:64 + TPC * E].rearrange("p (t e) -> p t e", e=E), onehot[:], ALU.mult))
                cg.link(nc.vector.tensor_reduce(col["pos"][:], pm[:], AX_X, ALU.add))
                cg.link(nc.vector.tensor_scalar(col["over"][:], col["pos"][:], float(CAP), float(NOWHERE), ALU.is_ge, ALU.mult))
                cg.link(nc.vector.tensor_scalar(col["slot"][:], col["m8"][:], -float(CAP), float(E * CAP), ALU.mult, ALU.add))
                cg.link(nc.vector.tensor_tensor(col["where"][:], col["slot"][:], col["pos"][:], ALU.add))
                cg.link(nc.vector.tensor_tensor(col["slot"][:], col["where"][:], col["over"][:], ALU.add))
                nc.vector.tensor_copy(slot_ids[:, bass.ds(TPC * c, TPC)], col["slot"][:]).then_inc(slots_ready, 1)
                cg.end()

            def w1_lo(e, js):
                for j in js:
                    if first(e) and j == NP // 2:
                        dve.wait_ge(lo_split, splits_before(0, "w1") + NP // 2)
                    split_lo(wA[HI][:, 1024 * j:1024 * j + 1024], wA[LO][:, 1024 * j:1024 * j + 1024], raw[:, j, :],
                             splits_before(e, "w1") + j + 1)

            dve.wait_ge(x_first, 16)
            t_statistics(0)
            for n in range(RING):
                attn_weights(n)
            dve.wait_ge(small_in, 32)
            nc.vector.tensor_scalar(scale64[:], scale_in[:], WSCALE, None, ALU.mult).then_inc(small_split, 1)
            dve.wait_ge(small_split, 1)
            dve.wait_ge(x_rest, 16)
            dve.wait_ge(consts, 1)
            for c in range(1, NCH):
                t_statistics(c)
            scan_up(0)
            scan_down(0)
            gated(0)
            for c in range(1, NCH):
                scan_up(c, {2: lambda: rms_scale(c - 1),
                            4: lambda: x1_tile(c - 1, 0),
                            8: lambda: x1_tile(c - 1, 1),
                            16: lambda: x1_tile(c - 1, 2),
                            64: lambda: x1_tile(c - 1, 3)})
                scan_down(c, {32: lambda: rstd_payload(c - 1), 2: lambda: route(c - 1)})
                gated(c)
                place(c - 1)
            rms_scale(NCH - 1)
            for t in range(TPC):
                x1_tile(NCH - 1, t)
            w1_lo(0, range(NP // 2, NP))
            rstd_payload(NCH - 1)
            route(NCH - 1)
            place(NCH - 1)

            def e_normalise(e):
                for t in range(CT):
                    row = tile_at(CT * e + t)
                    wait(dve, nrm["e"]["lo"], CT * e)
                    nc.vector.tensor_scalar(xn[:, t, :], row[:, 0:D], row[:, MEAN:MEAN + 1], row[:, RSTD:RSTD + 1],
                                            ALU.subtract, ALU.mult).then_inc(nrm["e"]["xn"], 1)
                for t in range(CT):
                    dve.wait_ge(nrm["e"]["hi"], CT * e + t + 1)
                    nc.vector.tensor_tensor(xs[:, t, LO, :], xn[:, t, :], xs[:, t, HI, :], ALU.subtract).then_inc(nrm["e"]["lo"], 1)

            def combine(e, t):
                row = tile_at(CT * e + t)
                wait(dve, rows_out[t], 16 * e)
                nc.vector.tensor_copy(row_ids[:, t:t + 1], row[:, ID:ID + 1].bitcast(U32)).then_inc(ids_ready, 1)
                dve.wait_ge(down_done, CT * e + t + 1)
                dve.wait_ge(ids_ready, CT * e + t + 1)
                nc.vector.scalar_tensor_tensor(out=done_rows[:, t, :], in0=wps[:, t, :], scalar=row[:, GATE:GATE + 1], in1=row[:, 0:D],
                                               op0=ALU.mult, op1=ALU.add).then_inc(combined, 1)

            def expert(e, last):
                for j in range(NP):
                    dve.wait_ge(gel_ready, NP * e + j + 1)
                    g = gel[:, j % 2, :].rearrange("p (a n) -> p a n", a=2)
                    nc.vector.tensor_scalar(hid[:, HI, 2 * j:2 * j + 2, :], g, WSCALE, None, ALU.mult).then_inc(hhi_ready, 1)
                    split_lo(wB[HI][:, 1024 * j:1024 * j + 1024], wB[LO][:, 1024 * j:1024 * j + 1024], raw[:, j, :],
                             splits_before(e, "w2") + j + 1)
                    dve.wait_ge(hhi_ready, NP * e + j + 1)
                    nc.vector.scalar_tensor_tensor(out=hid[:, LO, 2 * j:2 * j + 2, :], in0=g, scalar=WSCALE, in1=hid[:, HI, 2 * j:2 * j + 2, :],
                                                   op0=ALU.mult, op1=ALU.subtract).then_inc(hlo_ready, 1)
                if not last:
                    e_normalise(e + 1)
                    w1_lo(e + 1, range(NP // 2))
                combine(e, 0)
                if not last:
                    w1_lo(e + 1, range(NP // 2, NP))
                combine(e, 1)

            dve.wait_ge(e_first, 16)
            e_normalise(0)
            dve.wait_ge(e_rest, 16)
            expert(0, False)
            with dve.Fori(1, E - 1) as e:
                expert(e, False)
            expert(E - 1, True)

        @block.tensor
        def _(pe):
            def turn(part, u, tiles, free):
                for t in range(tiles):
                    pe.wait_ge(nrm[part]["lo"], tiles * u + t + 1)
                    free(t)
                    for hl in range(2):
                        for k in range(KD):
                            last = nc.tensor.transpose(tps16[:, t % 2, hl, k, :], xs[:, t, hl, k * P:(k + 1) * P], ident[:])
                    last.then_inc(nrm[part]["turned"], 1)

            def part_t(c):
                def free(t):
                    if t >= 2:
                        pe.wait_ge(nrm["t"]["copied"], TPC * c + t - 1)
                    elif not first(c):
                        pe.wait_ge(nrm["t"]["copied"], TPC * c)
                        wait(pe, nrm["b"]["copied"], TPC * (c - 3))
                turn("t", c, TPC, free)

            def project(c, w, m, done):
                half = c & 1
                n = 0
                for k in range(KD):
                    for a, b in PASSES:
                        last = nc.tensor.matmul(zps[:, w, :], proj[a][:, w, k, m * P:(m + 1) * P],
                                                xT[:, bass.ds(half, 1), b, k, :].rearrange("p c n -> p (c n)"),
                                                start=(n == 0), stop=(n == 3 * KD - 1))
                        n += 1
                last.then_inc(done, 1)

            def z_f(c, m):
                if first(c) and m == 0:
                    pe.wait_ge(lo_split, 2)
                if m == 0:
                    pe.wait_ge(nrm["t"]["copied"], TPC * (c + 1))
                wait(pe, f_ready, 4 * c + m)
                project(c, 0, m, zf_done)

            def z_c(c, m):
                if first(c) and m == 0:
                    pe.wait_ge(lo_split, 4)
                wait(pe, c_ready, 4 * c + m)
                project(c, 1, m, zc_done)

            def z_r(c, m):
                if first(c) and m == 0:
                    pe.wait_ge(lo_split, 6)
                wait(pe, r_ready, 4 * c + m)
                project(c, 2, m, zr_done)

            def sums_of_squares(c):
                pe.wait_ge(hsq_ready, 4 * (c + 1))
                if c < NCH - 1:
                    wait(pe, slots_ready, c)
                else:
                    pe.wait_ge(f_ready, KD * NCH)
                for t in range(TPC):
                    for m in range(KD):
                        last = nc.tensor.matmul(sums_bank(c)[:, t:t + 1], hsq[:, m, t * P:(t + 1) * P], ones32[:], start=(m == 0), stop=(m == KD - 1))
                last.then_inc(rms_done, 1)

            def out_projection(c, *tiles):
                for t in tiles:
                    if t == 0:
                        pe.wait_ge(plo_ready, 4 * (c + 1))
                        pe.wait_ge(lo_split, RING)
                    wait(pe, x1_ready, TPC * c + t - 1)
                    n = 0
                    for m in range(KD):
                        for a, b in PASSES:
                            last = nc.tensor.matmul(wps[:, t % 2, :], pT[a][:, m, t * P:(t + 1) * P], proj[b][:, 3, m, :],
                                                    start=(n == 0), stop=(n == 3 * KD - 1))
                            n += 1
                    last.then_inc(wo_done, 1)

            def logits(c, *tiles):
                for t in tiles:
                    pe.wait_ge(nrm["b"]["copied"], TPC * c + t + 1)
                    if t == 0:
                        pe.wait_ge(rms_var, c + 1)
                        wait(pe, slots_ready, c)
                    for k in range(KD):
                        last = nc.tensor.matmul(sps[:, 0, 32 + t * E:32 + (t + 1) * E], x1T[:, t % 2, k, :], wg_in[:, k, :],
                                                start=(k == 0), stop=(k == KD - 1))
                    if t == TPC - 1:
                        last.then_inc(logits_done, 1)

            def turn_x1(c, *tiles):
                for t in tiles:
                    pe.wait_ge(nrm["b"]["xn"], TPC * c + t + 1)
                    wait(pe, nrm["b"]["copied"], TPC * c + t - 1)
                    if t < 2:
                        pe.wait_ge(nrm["t"]["copied"], TPC * min(c + 4, NCH))
                    for k in range(KD):
                        last = nc.tensor.transpose(tps32[:, t % 2, k, :], x1n[:, t, k * P:(k + 1) * P], ident32[:])
                    last.then_inc(nrm["b"]["turned"], 1)

            def positions(c):
                pe.wait_ge(onehot_ready, c + 1)
                nc.tensor.matmul(sps[:, 0, 64:64 + TPC * E], earlier[:], onehot[:].rearrange("p t e -> p (t e)"), start=True, stop=False)
                nc.tensor.matmul(sps[:, 0, 64:64 + TPC * E], ones16[:], before[:, 0:TPC, :].rearrange("p t e -> p (t e)"),
                                 start=False, stop=True).then_inc(pos_done, 1)

            def z(c, *ms):
                for m in ms:
                    z_f(c, m)
                    z_c(c, m)
                    z_r(c, m)

            pe.wait_ge(consts, 1)
            pe.wait_ge(small_in, 32)
            part_t(0)
            z(0, 0, 1)
            part_t(1)
            z(0, 2, 3)
            z(1, 0, 1)
            part_t(2)
            z(1, 2, 3)
            for c in range(2, NCH):
                sums_of_squares(c - 2)
                out_projection(c - 2, 0, 1, 2, 3)
                if c + 1 < NCH:
                    part_t(c + 1)
                turn_x1(c - 2, 0, 1)
                z(c, 0)
                logits(c - 2, 0, 1)
                turn_x1(c - 2, 2, 3)
                z_f(c, 1)
                logits(c - 2, 2, 3)
                z_c(c, 1)
                z_r(c, 1)
                positions(c - 2)
                z(c, 2, 3)
            for c in range(NCH - 2, NCH):
                sums_of_squares(c)
                out_projection(c, 0, 1, 2)
                turn_x1(c, 0)
                out_projection(c, 3)
                turn_x1(c, 1)
                logits(c, 0)
                turn_x1(c, 2)
                logits(c, 1)
                turn_x1(c, 3)
                logits(c, 2, 3)
                positions(c)

            def turn_expert(e):
                if isinstance(e, int) and e == 0:
                    turn("e", e, CT, lambda t: None)
                else:
                    turn("e", e, CT, lambda t: pe.wait_ge(nrm["e"]["copied"], CT * e))

            def up(e, j):
                pe.wait_ge(lo_split, splits_before(e, "w1") + j + 1)
                if j == 0:
                    pe.wait_ge(nrm["e"]["copied"], CT * (e + 1))
                wait(pe, gel_ready, NP * e + (j - 1 if j < 2 else j - 2))
                for f in range(2):
                    n = 0
                    for k in range(KD):
                        for a, b in PASSES:
                            last = nc.tensor.matmul(zps[:, j % 3, f * CAP:(f + 1) * CAP], w1s[a][:, j, k, f * P:(f + 1) * P], xTe[:, b, k, :],
                                                    start=(n == 0), stop=(n == 3 * KD - 1))
                            n += 1
                last.then_inc(up_done, 1)

            def down(e, t, turns):
                wait(pe, combined, CT * (e - 1) + t + 1)
                n = 0
                for j in range(NP):
                    if t == 0:
                        pe.wait_ge(lo_split, splits_before(e, "w2") + j + 1)
                        pe.wait_ge(hlo_ready, NP * e + j + 1)
                    for f in range(2):
                        for a, b in PASSES:
                            last = nc.tensor.matmul(wps[:, t, :], hid[:, a, 2 * j + f, t * P:(t + 1) * P], w2s[b][:, j, f, :],
                                                    start=(n == 0), stop=(n == 6 * NP - 1))
                            n += 1
                last.then_inc(down_done, 1)

            def expert(e, last):
                for j in range(NP):
                    up(e, j)
                down(e, 0, False)
                if not last:
                    turn_expert(e + 1)
                down(e, 1, False)

            turn_expert(0)
            expert(0, False)
            with pe.Fori(1, E - 1) as e:
                expert(e, False)
            expert(E - 1, True)


_INS = ["L0_attn_x", "L0_attn_Wr", "L0_attn_Wf", "L0_attn_Wc", "L0_attn_Wo", "L0_attn_ln_scale", "L0_ffn_w_gate", "L0_ffn_w1", "L0_ffn_w2"]
_OUTS = [((2, 1024, 512), "float32")]


def kernel(**inputs):
    import numpy as _np
    import concourse.bacc as _bacc
    from concourse import mybir as _mybir
    from concourse.bass_utils import run_bass_kernel_spmd as _run

    nc = _bacc.Bacc("TRN2", target_bir_lowering=False, num_devices=1)
    arrays, args = {}, []
    for name in _INS:
        a = _np.ascontiguousarray(inputs[name])
        arrays[f"in_{name}_dram"] = a
        args.append(nc.dram_tensor(f"in_{name}_dram", a.shape, _mybir.dt.from_np(a.dtype), kind="ExternalInput").ap())
    for i, (shape, dtype) in enumerate(_OUTS):
        dt = _mybir.dt.from_np(_np.dtype(dtype))
        args.append(nc.dram_tensor(f"out_{i}_dram", shape, dt, kind="ExternalOutput").ap())
    recurrent_block_with_experts(nc, *args)
    r = _run(nc, [arrays], core_ids=[0])
    return r.results[0]["out_0_dram"]
```

```python
from contextlib import ExitStack

import concourse.bass as bass
from concourse import mybir

P = 128
F32 = mybir.dt.float32
F16 = mybir.dt.float16
U32 = mybir.dt.uint32
ALU = mybir.AluOpType
ACT = mybir.ActivationFunctionType
AX_X = mybir.AxisListType.X

EPS = 1e-5
WSCALE = 64.0
UNSCALE = WSCALE**-2
HI, LO = 0, 1
PASSES = ((HI, HI), (HI, LO), (LO, HI))


class Chain:

    def __init__(self, sem, engine, per_unit):
        self.sem, self.engine, self.per_unit, self.done = sem, engine, per_unit, 0

    def start(self, unit):
        self.base, self.done = unit * self.per_unit, 0

    def step(self, instruction):
        instruction.then_inc(self.sem, 1)
        self.done += 1
        return self.base + self.done

    def after(self, value):
        self.engine.wait_ge(self.sem, value)

    def link(self, instruction):
        self.after(self.step(instruction))

    def end(self):
        assert self.done == self.per_unit, (self.sem, self.done)


def recurrent_block_with_experts(nc, x, Wr, Wf, Wc, Wo, ln_scale, w_gate, w1, w2, out):
    B, S, D = x.shape
    E, _, F = w1.shape
    TOK = B * S
    CAP = TOK // E
    CH = 512
    NCH = TOK // CH
    TPC = CH // P
    NT = TOK // P
    KD = D // P
    FW = 256
    NP = F // FW
    CT = CAP // P
    RING = 8
    SLOT = KD * FW
    AW = 4
    MEAN, RSTD, GATE, ID = D, D + 1, D + 2, D + 3
    XW = D + 4
    NOWHERE = 1 << 20
    TREE = 3 * 9 + 3 * 10 - 1
    ROUTING = 17
    assert AW * KD * D == RING * SLOT and NP == RING and S % CH == 0 and CT == 2
    CHUNKS_PER_SEQ = S // CH
    assert CHUNKS_PER_SEQ == 2

    x_rows = x.rearrange("b s d -> (b s) d")
    out_rows = out.rearrange("b s d -> (b s) d")
    x_tiles = x_rows.rearrange("(t p) d -> p t d", p=P)
    out_tiles = out_rows.rearrange("(t p) d -> p t d", p=P)
    table = nc.dram_tensor("expert_rows", (E * CAP, XW), F32, kind="Internal").ap()
    table_tiles = table.rearrange("(t p) d -> p t d", p=P)
    w1_chunks = w1.rearrange("e (k p) (j n) -> e j p k n", p=P, j=NP)
    w2_chunks = w2.rearrange("e (j a p) n -> e j p a n", p=P, j=NP)

    with ExitStack() as ctx:
        def sb(name, shape, dt=F32):
            return ctx.enter_context(nc.sbuf_tensor(name, shape, dt))

        def sem(name):
            return ctx.enter_context(nc.semaphore(name))

        rows = sb("rows", [P, NT, XW])
        raw = sb("raw", [P, RING, SLOT])
        wB = [sb("wB_hi", [P, RING * SLOT], F16), sb("wB_lo", [P, RING * SLOT], F16)]
        wA = [sb("wA_hi", [P, RING * SLOT], F16), sb("wA_lo", [P, RING * SLOT], F16)]
        proj = [w[:].rearrange("p (w k n) -> p w k n", w=AW, k=KD) for w in wB]
        w2s = [w[:].rearrange("p (j a n) -> p j a n", j=NP, a=2) for w in wB]
        w1s = [w[:].rearrange("p (j k n) -> p j k n", j=NP, k=KD) for w in wA]
        xT = sb("xT", [P, 2, 2, KD, CH], F16)
        xTe = xT[:, 0].rearrange("p h k n -> p (h k n)")[:, 0:2 * KD * CAP].rearrange("p (h k n) -> p h k n", h=2, k=KD)
        f_all = wA[HI][:].bitcast(F32).rearrange("p (c m n) -> p c m n", c=2, m=KD)
        r_all = wA[LO][:].bitcast(F32).rearrange("p (c m n) -> p c m n", c=2, m=KD)
        state = sb("state", [P, 2, KD, 1 + CH])
        hid = state[:].rearrange("p c m n -> p (c m n)").bitcast(F16)[:, 0:2 * F // P * CAP].rearrange("p (h f n) -> p h f n", h=2, n=CAP)
        tmp = sb("tmp", [P, KD, CH // 2])
        gel = tmp[:].rearrange("p m n -> p (m n)").rearrange("p (b n) -> p b n", b=2)
        hsq = sb("hsq", [P, KD, CH])
        pT = [sb("pT_hi", [P, KD, CH], F16), sb("pT_lo", [P, KD, CH], F16)]
        done_rows = hsq[:, 0:2, :]
        xn = sb("xn", [P, 2, D])
        xs = sb("xs", [P, TPC, 2, D], F16)
        x1n = sb("x1n", [P, TPC, D])
        x1T = sb("x1T", [P, 2, KD, P])
        fill = x1T[:].rearrange("p b k n -> p (b k n)")[:, 0:XW]
        ident = sb("ident", [P, P], F16)
        ident32 = sb("ident32", [P, P])
        earlier = sb("earlier", [P, P], F16)
        ones16 = sb("ones16", [P, P], F16)
        ones32 = sb("ones32", [P, 1])
        neg_half = sb("neg_half", [P, TPC])
        rank = sb("rank", [P, TPC, E])
        scale64 = sb("scale64", [P, KD])
        scale_in = sb("scale_in", [P, KD])
        wg_in = sb("wg_in", [P, KD, E])
        keep = sb("keep", [P, NCH])
        width = {"t": NT, "b": TPC, "r": TPC}
        st = {n: sb(f"st_{n}", [P, TPC, 6]) for n in "tb"}
        mv = sb("mv", [P, TPC, 2])
        rs = {n: sb(f"rs_{n}", [P, width[n]]) for n in "tbr"}
        shift = {n: sb(f"shift_{n}", [P, width[n]]) for n in "tb"}
        small = {n: sb(f"sm_{n}", [P, TPC, E]) for n in ("lg", "d", "sg", "om", "rc", "eq")}
        small["ex"], small["pm"] = small["om"], small["lg"]
        col = {n: sb(f"col_{n}", [P, TPC]) for n in ("max", "ms", "sum", "gate", "m8", "pos", "slot", "over", "where")}
        onehot = sb("onehot", [P, TPC, E], F16)
        before = sb("before", [P, E], F16)
        chunk_count = sb("chunk_count", [P, E])
        slot_ids = sb("slot_ids", [P, NT], U32)
        row_ids = sb("row_ids", [P, CT], U32)

        def bank(name, n, dt=F32):
            return ctx.enter_context(nc.psum_tensor(name, [P, n, 2048 // (4 if dt == F32 else 2)], dt))

        zps = bank("zps", 3)
        sps = bank("sps", 1)
        tps = bank("tps", 2, F16)
        wps = bank("wps", 2)
        tps16 = tps[:].rearrange("p b (h k n) -> p b h k n", h=2, k=KD)
        tps32 = tps[:].bitcast(F32).rearrange("p b (k n) -> p b k n", k=KD)

        X_PARTS = [(0, TPC // 2), (TPC // 2, TPC)] + [(TPC * c, TPC * (c + 1)) for c in range(1, NCH)]
        x_in, small_in = [sem(f"x_in{i}") for i in range(len(X_PARTS))], sem("small_in")
        raw_in = [sem(f"raw_in{i}") for i in range(RING)]
        hi_split, lo_split = sem("hi_split"), sem("lo_split")
        small_split, scaled = sem("small_split"), sem("scaled")
        consts, setup = sem("consts"), sem("setup")
        table_clear, scattered, base_out = sem("table_clear"), sem("scattered"), sem("base_out")
        nrm = {p: {n: sem(f"{p}_{n}") for n in ("var", "rstd", "xn", "hi", "lo", "turned", "copied")} for p in "tbe"}
        chain_s, chain_n, chain_g = sem("chain_s"), sem("chain_n"), sem("chain_g")
        zf_done, zc_done, zr_done = sem("zf_done"), sem("zc_done"), sem("zr_done")
        tanh_ready, f_ready, c_ready, r_ready = sem("tanh_ready"), sem("f_ready"), sem("c_ready"), sem("r_ready")
        tree_step, states_ready, hsq_ready, hsum_ready, phi_ready, p_ready, plo_ready = (
            sem(n) for n in ("tree_step", "states_ready", "hsq_ready", "hsum_ready", "phi_ready", "p_ready", "plo_ready"))
        rms_done, rms_var, rms_rstd, wo_done, y_ready, x1_ready = (sem(n) for n in ("rms_done", "rms_var", "rms_rstd", "wo_done", "y_ready", "x1_ready"))
        logits_done, diff_ready, sig_ready, onehot_ready, pos_done, slots_ready = (
            sem(n) for n in ("logits_done", "diff_ready", "sig_ready", "onehot_ready", "pos_done", "slots_ready"))
        e_first, e_rest = sem("e_first"), sem("e_rest")
        up_done, gel_ready, hhi_ready, hlo_ready, down_done = (sem(n) for n in ("up_done", "gel_ready", "hhi_ready", "hlo_ready", "down_done"))
        ids_ready, combined, rows_out = sem("ids_ready"), sem("combined"), [sem(f"rows_out{t}") for t in range(CT)]

        block = ctx.enter_context(nc.Block())

        def wait(eng, s, value):
            if not isinstance(value, int) or value > 0:
                eng.wait_ge(s, value)

        def wo_bank(t):
            return wps[:, (t + 1) % 2, :]

        def first(unit):
            return isinstance(unit, int) and unit == 0

        def tile_at(t):
            return rows[:, bass.ds(t, 1), :].rearrange("p a d -> p (a d)")

        def splits_before(e, matrix):
            return RING * (1 + 2 * e + (matrix == "w2"))

        def raw_wait(eng, e, matrix, j):
            eng.wait_ge(raw_in[j], 16 * (splits_before(e, matrix) // RING + 1) if isinstance(e, int)
                        else 32 * e + (48 if matrix == "w2" else 32))

        @block.sync
        def _(sp):
            def load_x(i):
                start, stop = X_PARTS[i]
                sp.dma_start(rows[:, start:stop, 0:D], x_tiles[:, start:stop, :]).then_inc(x_in[i], 16)

            load_x(0)
            load_x(1)
            for i, w in enumerate((Wf, Wc, Wr, Wo)):
                w_in = w.rearrange("(k p) n -> p k n", p=P)
                for half in range(2):
                    sp.dma_start(raw[:, 2 * i + half, :].rearrange("p (k n) -> p k n", k=2),
                                 w_in[:, 2 * half:2 * half + 2, :]).then_inc(raw_in[2 * i + half], 16)
                if i == 0:
                    with nc.allow_non_contiguous_dma(reason="2 KB in all"):
                        sp.dma_start(scale_in[:], ln_scale.rearrange("(k p) -> p k", p=P)).then_inc(small_in, 16)
                    sp.dma_start(wg_in[:], w_gate.rearrange("(k p) e -> p k e", p=P)).then_inc(small_in, 16)
                if i == 2:
                    for part in range(2, len(X_PARTS)):
                        load_x(part)
            sp.wait_ge(consts, 1)
            for t in range(NT):
                sp.dma_start(table_tiles[:, t, :], fill).then_inc(table_clear, 16)

            def load(e, matrix):
                for j in range(NP):
                    sp.wait_ge(lo_split, splits_before(e, matrix) - RING + j + 1)
                    if matrix == "w1":
                        src = w1_chunks[bass.ds(e, 1), j].rearrange("e p k n -> p (e k) n")
                        dst = raw[:, j, :].rearrange("p (k n) -> p k n", k=KD)
                    else:
                        src = w2_chunks[bass.ds(e, 1), j].rearrange("e p a n -> p (e a) n")
                        dst = raw[:, j, :].rearrange("p (a n) -> p a n", a=2)
                    sp.dma_start(dst, src).then_inc(raw_in[j], 16)

            load(0, "w1")
            load(0, "w2")
            sp.wait_ge(scattered, 16 * NT)
            sp.wait_ge(base_out, 16 * NCH)
            sp.dma_start(rows[:, 0:CT, :], table_tiles[:, 0:CT, :]).then_inc(e_first, 16)
            sp.dma_start(rows[:, CT:NT, :], table_tiles[:, CT:NT, :]).then_inc(e_rest, 16)
            with sp.Fori(1, E) as e:
                load(e, "w1")
                load(e, "w2")

        @block.gpsimd
        def _(pool):
            steps = [0]

            def made(instruction):
                steps[0] += 1
                instruction.then_inc(setup, 1)
                return steps[0]

            made(nc.gpsimd.memset(fill, 0.0))
            made(nc.gpsimd.memset(ident[:], 1.0))
            made(nc.gpsimd.memset(earlier[:], 1.0))
            made(nc.gpsimd.memset(ones16[:], 1.0))
            made(nc.gpsimd.memset(ones32[:], 1.0))
            made(nc.gpsimd.memset(neg_half[:], -0.5))
            made(nc.gpsimd.memset(state[:, 0, :, 0:1], 0.0))
            made(nc.gpsimd.memset(ident32[:], 1.0))
            made(nc.gpsimd.memset(keep[:], 1.0))
            made(nc.gpsimd.memset(before[:], 0.0))
            pool.wait_ge(setup, steps[0])
            made(nc.gpsimd.iota(fill[:, ID:ID + 1].bitcast(U32), pattern=[[0, 1]], base=NOWHERE, channel_multiplier=0))
            for e in range(E):
                made(nc.gpsimd.memset(rank[:, :, e], float(E - e)))
            for c in range(0, NCH, CHUNKS_PER_SEQ):
                made(nc.gpsimd.memset(keep[:, c:c + 1], 0.0))
            made(nc.gpsimd.affine_select(out=ident[:], in_=ident[:], compare_op=ALU.is_equal, fill=0.0,
                                         base=0, pattern=[[-1, P]], channel_multiplier=1))
            made(nc.gpsimd.affine_select(out=ident32[:], in_=ident32[:], compare_op=ALU.is_equal, fill=0.0,
                                         base=0, pattern=[[-1, P]], channel_multiplier=1))
            made(nc.gpsimd.affine_select(out=earlier[:], in_=earlier[:], compare_op=ALU.is_gt, fill=0.0,
                                         base=0, pattern=[[1, P]], channel_multiplier=-1))
            pool.wait_ge(setup, steps[0])
            for t in range(NT):
                made(nc.gpsimd.iota(rows[:, t, ID:ID + 1].bitcast(U32), pattern=[[0, 1]], base=t * P, channel_multiplier=1))
            pool.wait_ge(setup, steps[0])
            nc.gpsimd.memset(slot_ids[:], 0).then_inc(consts, 1)

            def power(part, count, tiles):
                pool.wait_ge(nrm[part]["var"], count)
                made(nc.gpsimd.tensor_tensor(rs[part][:, tiles], rs[part][:, tiles], neg_half[:, 0:tiles.stop - tiles.start], ALU.pow))
                pool.wait_ge(setup, steps[0])
                nc.gpsimd.tensor_tensor(shift[part][:, tiles], shift[part][:, tiles], rs[part][:, tiles], ALU.mult).then_inc(nrm[part]["rstd"], 1)

            def t_lo(c):
                for t in range(TPC):
                    pool.wait_ge(nrm["t"]["hi"], TPC * c + t + 1)
                    nc.gpsimd.tensor_tensor(xs[:, t, LO, :], xn[:, t % 2, :], xs[:, t, HI, :], ALU.subtract).then_inc(nrm["t"]["lo"], 1)

            def rms_norm(c):
                for m in range(1, KD):
                    pool.wait_ge(hsq_ready, KD * c + m + 1)
                    last = nc.gpsimd.tensor_tensor(hsq[:, 0, :], hsq[:, 0, :], hsq[:, m, :], ALU.add)
                    if m < KD - 1:
                        made(last)
                        pool.wait_ge(setup, steps[0])
                last.then_inc(hsum_ready, 1)
                pool.wait_ge(rms_var, c + 1)
                nc.gpsimd.tensor_tensor(rs["r"][:], rs["r"][:], neg_half[:], ALU.pow).then_inc(rms_rstd, 1)

            def add_y(c, t):
                pool.wait_ge(y_ready, TPC * c + t + 1)
                row = rows[:, TPC * c + t, 0:D]
                nc.gpsimd.tensor_tensor(row, row, x1n[:, t, :], ALU.add).then_inc(x1_ready, 1)

            def second_norm(c):
                def norm_power(t):
                    power("b", TPC * c + t + 1, slice(t, t + 1))

                if c < NCH - 1:
                    add_y(c, 0)
                    add_y(c, 1)
                    add_y(c, 2)
                    norm_power(0)
                    add_y(c, 3)
                    norm_power(1)
                    norm_power(2)
                    norm_power(3)
                else:
                    for t in range(TPC):
                        norm_power(t)
                pool.wait_ge(x1_ready, TPC * (c + 1))
                pool.dma_start(out_tiles[:, TPC * c:TPC * c + TPC, :], rows[:, TPC * c:TPC * c + TPC, 0:D]).then_inc(base_out, 16)

            def scatter(c):
                pool.wait_ge(slots_ready, c + 1)
                if c == 0:
                    pool.wait_ge(table_clear, 16 * NT)
                for t in range(TPC * c, TPC * c + TPC):
                    pool.indirect_dma_start(
                        out=table, out_offset=bass.IndirectOffsetOnAxis(ap=slot_ids[:, t:t + 1], axis=0),
                        in_=rows[:, t, :], in_offset=None, bounds_check=E * CAP - 1, oob_is_err=False).then_inc(scattered, 16)

            def w1_lo(j):
                pool.wait_ge(scaled, j + 1)
                nc.gpsimd.tensor_tensor(wA[LO][:, SLOT * j:SLOT * j + SLOT], raw[:, j, :], wA[HI][:, SLOT * j:SLOT * j + SLOT],
                                        ALU.subtract).then_inc(lo_split, 1)

            for i, (start, stop) in enumerate(X_PARTS):
                power("t", i + 1, slice(start, stop))
                if start == TPC:
                    t_lo(1)
            for c in range(2, NCH - 1):
                t_lo(c)
            rms_norm(0)
            for c in range(1, NCH):
                second_norm(c - 1)
                if c == 1:
                    t_lo(NCH - 1)
                else:
                    scatter(c - 2)
                if c == NCH - 1:
                    for j in range(NP // 2 - 1):
                        w1_lo(j)
                rms_norm(c)
            w1_lo(NP // 2 - 1)
            second_norm(NCH - 1)
            scatter(NCH - 2)
            scatter(NCH - 1)

            for e in range(E):
                for t in range(CT):
                    pool.wait_ge(combined, CT * e + t + 1)
                    pool.indirect_dma_start(
                        out=out_rows, out_offset=bass.IndirectOffsetOnAxis(ap=row_ids[:, t:t + 1], axis=0),
                        in_=done_rows[:, t, :], in_offset=None, bounds_check=TOK - 1, oob_is_err=False).then_inc(rows_out[t], 16)
            for t in range(CT):
                pool.wait_ge(rows_out[t], 16 * E)

        @block.scalar
        def _(act):
            def attn_weights(n):
                act.wait_ge(raw_in[n], 16)
                nc.scalar.activation(wB[HI][:, SLOT * n:SLOT * n + SLOT], raw[:, n, :], ACT.Copy, scale=WSCALE).then_inc(hi_split, 1)

            def normal(u):
                for t in range(TPC):
                    if t == 0:
                        act.wait_ge(nrm["t"]["rstd"], u + 2)
                        wait(act, nrm["t"]["turned"], TPC * u)
                    wait(act, nrm["t"]["lo"], TPC * u + max(t - 1, 0))
                    for dst in (xn[:, t % 2, :], xs[:, t, HI, :]):
                        last = nc.scalar.activation(dst, rows[:, TPC * u + t, 0:D], ACT.Identity, scale=rs["t"][:, TPC * u + t:TPC * u + t + 1],
                                                    bias=shift["t"][:, TPC * u + t:TPC * u + t + 1])
                    last.then_inc(nrm["t"]["hi"], 1)

            def take_y(c, t):
                act.wait_ge(wo_done, TPC * c + t + 1)
                act.wait_ge(rms_rstd, c + 1)
                wait(act, nrm["b"]["turned"], TPC * (c - 1) + t + 1)
                nc.scalar.activation(x1n[:, t, :], wo_bank(t), ACT.Identity, scale=rs["r"][:, t:t + 1]).then_inc(y_ready, 1)

            def normal_x1(c, *tiles):
                for t in tiles:
                    act.wait_ge(nrm["b"]["rstd"], TPC * c + t + 1)
                    wait(act, nrm["b"]["turned"], TPC * (c - 1) + t + 1)
                    nc.scalar.activation(x1n[:, t, :], rows[:, TPC * c + t, 0:D], ACT.Identity, scale=rs["b"][:, t:t + 1],
                                         bias=shift["b"][:, t:t + 1]).then_inc(nrm["b"]["xn"], 1)

            def copy_turned(part, u, tiles, dst, src, some=None):
                for t in some or range(tiles):
                    act.wait_ge(nrm[part]["turned"], tiles * u + t + 1)
                    nc.scalar.activation(dst(t), src[:, t % 2], ACT.Copy).then_inc(nrm[part]["copied"], 1)

            def t_copies(c, *some):
                wait(act, zr_done, KD * (c - 1))
                copy_turned("t", c, TPC, lambda t: xT[:, c % 2, :, :, t * P:(t + 1) * P], tps16, some)

            def gates(c, m):
                act.wait_ge(zf_done, KD * c + m + 1)
                if m == 0:
                    wait(act, p_ready, KD * (c - 1))
                    wait(act, plo_ready, KD * (c - 1))
                nc.scalar.activation(zps[:, 0, :], zps[:, 0, :], ACT.Tanh, scale=UNSCALE / 2).then_inc(tanh_ready, 1)
                act.wait_ge(zc_done, KD * c + m + 1)
                nc.scalar.activation(state[:, c % 2, m, 1:1 + CH], zps[:, 1, :], ACT.Silu, scale=UNSCALE).then_inc(c_ready, 1)
                act.wait_ge(tanh_ready, KD * c + m + 1)
                nc.scalar.activation(f_all[:, c % 2, m, :], zps[:, 0, :], ACT.Copy, scale=0.5, bias=0.5).then_inc(f_ready, 1)
                act.wait_ge(zr_done, KD * c + m + 1)
                nc.scalar.activation(r_all[:, c % 2, m, :], zps[:, 2, :], ACT.Silu, scale=UNSCALE).then_inc(r_ready, 1)

            def squares(c):
                act.wait_ge(states_ready, c + 1)
                wait(act, rms_done, c)
                for m in range(KD):
                    nc.scalar.activation(hsq[:, m, :], state[:, c % 2, m, 1:1 + CH], ACT.Square).then_inc(hsq_ready, 1)

            def p_hi(c):
                for m in range(KD):
                    act.wait_ge(p_ready, KD * c + m + 1)
                    if m == 0:
                        wait(act, wo_done, TPC * c)
                    nc.scalar.activation(pT[HI][:, m, :], r_all[:, c % 2, m, :], ACT.Copy).then_inc(phi_ready, 1)

            def tanh_of_diff(c):
                act.wait_ge(diff_ready, c + 1)
                nc.scalar.activation(small["sg"][:], small["d"][:], ACT.Tanh, scale=0.5 / WSCALE).then_inc(sig_ready, 1)

            def b_copies(c, *some):
                copy_turned("b", c, TPC, lambda t: x1T[:, t % 2], tps32, some)

            def w1_hi(e, js=range(NP)):
                for j in js:
                    raw_wait(act, e, "w1", j)
                    if j == 0:
                        wait(act, up_done, NP * e)
                    if first(e) and j in (0, NP // 2):
                        act.wait_ge(plo_ready, KD * (NCH - 1 if j == 0 else NCH))
                    nc.scalar.activation(wA[HI][:, SLOT * j:SLOT * j + SLOT], raw[:, j, :], ACT.Copy, scale=WSCALE).then_inc(hi_split, 1)
                    if first(e) and j < NP // 2:
                        nc.scalar.activation(raw[:, j, :], raw[:, j, :], ACT.Copy, scale=WSCALE).then_inc(scaled, 1)

            def expert_hi(e):
                for t in range(CT):
                    act.wait_ge(nrm["e"]["xn"], CT * e + t + 1)
                    if t == 0:
                        act.wait_ge(nrm["t"]["turned"], NT)
                        wait(act, nrm["e"]["turned"], CT * e)
                    nc.scalar.activation(xs[:, t, HI, :], xn[:, t, :], ACT.Copy).then_inc(nrm["e"]["hi"], 1)

            def first_hi(t):
                act.wait_ge(nrm["t"]["xn"], t + 1)
                nc.scalar.activation(xs[:, t, HI, :], xn[:, t % 2, :], ACT.Copy).then_inc(nrm["t"]["hi"], 1)

            first_hi(0)
            first_hi(1)
            attn_weights(0)
            first_hi(2)
            t_copies(0, 0)
            first_hi(3)
            t_copies(0, 1)
            attn_weights(1)
            t_copies(0, 2, 3)
            for n in range(2, 6):
                attn_weights(n)
            gates(0, 0)
            normal(1)
            gates(0, 1)
            t_copies(1)
            attn_weights(6)
            attn_weights(7)
            gates(0, 2)
            gates(0, 3)
            gates(1, 0)
            normal(2)
            gates(1, 1)
            t_copies(2)
            gates(1, 2)
            squares(0)
            p_hi(0)
            gates(1, 3)
            act.wait_ge(table_clear, 16 * NT)
            for c in range(2, NCH):
                take_y(c - 2, 0)
                take_y(c - 2, 1)
                take_y(c - 2, 2)
                take_y(c - 2, 3)
                normal_x1(c - 2, 0, 1)
                gates(c, 0)
                b_copies(c - 2, 0, 1)
                normal_x1(c - 2, 2, 3)
                b_copies(c - 2, 2, 3)
                if c + 1 < NCH:
                    normal(c + 1)
                gates(c, 1)
                if c + 1 < NCH:
                    t_copies(c + 1)
                tanh_of_diff(c - 2)
                squares(c - 1)
                gates(c, 2)
                p_hi(c - 1)
                gates(c, 3)
            w1_hi(0, [0])
            take_y(NCH - 2, 0)
            w1_hi(0, [1])
            take_y(NCH - 2, 1)
            w1_hi(0, [2])
            take_y(NCH - 2, 2)
            w1_hi(0, [3])
            take_y(NCH - 2, 3)
            normal_x1(NCH - 2, 0)
            normal_x1(NCH - 2, 1)
            b_copies(NCH - 2, 0)
            normal_x1(NCH - 2, 2)
            b_copies(NCH - 2, 1)
            normal_x1(NCH - 2, 3)
            b_copies(NCH - 2, 2, 3)
            squares(NCH - 1)
            p_hi(NCH - 1)
            tanh_of_diff(NCH - 2)
            w1_hi(0, range(NP // 2, NP))
            for t in range(TPC):
                normal_x1(NCH - 1, t)
                if t >= 1:
                    b_copies(NCH - 1, t - 1)
            b_copies(NCH - 1, TPC - 1)
            tanh_of_diff(NCH - 1)

            def e_copies(e):
                copy_turned("e", e, CT, lambda t: xTe[:, :, :, t * P:(t + 1) * P], tps16)

            def expert(e, last):
                for j in range(NP):
                    act.wait_ge(up_done, NP * e + j + 1)
                    wait(act, hlo_ready, NP * e + j - 1)
                    nc.scalar.activation(gel[:, j % 2, :], zps[:, j % 3, :], ACT.Gelu_apprx_tanh, scale=UNSCALE).then_inc(gel_ready, 1)
                    raw_wait(act, e, "w2", j)
                    if j == 0:
                        wait(act, down_done, CT * e)
                        act.wait_ge(wo_done, NT)
                    nc.scalar.activation(wB[HI][:, SLOT * j:SLOT * j + SLOT], raw[:, j, :], ACT.Copy, scale=WSCALE).then_inc(hi_split, 1)
                if last:
                    return
                expert_hi(e + 1)
                act.wait_ge(up_done, NP * (e + 1))
                e_copies(e + 1)
                w1_hi(e + 1)

            expert_hi(0)
            e_copies(0)
            expert(0, False)
            with act.Fori(1, E - 1) as e:
                expert(e, False)
            expert(E - 1, True)

        @block.vector
        def _(dve):
            cs = Chain(chain_s, dve, 2)
            cn = Chain(chain_n, dve, 2)
            cg = Chain(chain_g, dve, ROUTING)

            def split_lo(hi, lo, src, count):
                dve.wait_ge(hi_split, count)
                nc.vector.scalar_tensor_tensor(out=lo, in0=src, scalar=WSCALE, in1=hi, op0=ALU.mult, op1=ALU.subtract).then_inc(lo_split, 1)

            def attn_weights(n):
                split_lo(wB[HI][:, SLOT * n:SLOT * n + SLOT], wB[LO][:, SLOT * n:SLOT * n + SLOT], raw[:, n, :], n + 1)

            def statistics(part, first_tile, count, source, moments):
                tiles = slice(first_tile, first_tile + count)
                for t in range(count):
                    nc.vector.bn_stats(st[part][:, t, :], source(t))
                nc.vector.drain()
                for t in range(count):
                    nc.vector.bn_aggr(moments[:, t, :], st[part][:, t, :])
                nc.vector.drain()
                nc.vector.tensor_scalar(shift[part][:, tiles], moments[:, :, 0], -1.0, None, ALU.mult)
                nc.vector.tensor_scalar(rs[part][:, tiles], moments[:, :, 1], EPS, UNSCALE, ALU.add, ALU.mult).then_inc(nrm[part]["var"], 1)

            def t_statistics(i):
                start, stop = X_PARTS[i]
                dve.wait_ge(x_in[i], 16)
                statistics("t", start, stop - start, lambda t: rows[:, start + t, 0:D], mv[:, start % TPC:start % TPC + stop - start, :])

            def first_xn(t):
                dve.wait_ge(nrm["t"]["rstd"], 1 + t // (TPC // 2))
                wait(dve, nrm["t"]["lo"], t - 1)
                nc.vector.tensor_scalar(xn[:, t % 2, :], rows[:, t, 0:D], mv[:, t, 0:1], rs["t"][:, t:t + 1],
                                        ALU.subtract, ALU.mult).then_inc(nrm["t"]["xn"], 1)

            def first_lo(t):
                dve.wait_ge(nrm["t"]["hi"], t + 1)
                nc.vector.tensor_tensor(xs[:, t, LO, :], xn[:, t % 2, :], xs[:, t, HI, :], ALU.subtract).then_inc(nrm["t"]["lo"], 1)

            tree = {"steps": 0}

            def link(c, instruction):
                tree["steps"] += 1
                instruction.then_inc(tree_step, 1)
                dve.wait_ge(tree_step, TREE * c + tree["steps"])

            def scan_start(c):
                tree["steps"] = 0
                cs.start(c)
                dve.wait_ge(f_ready, KD * (c + 1))
                dve.wait_ge(c_ready, KD * (c + 1))
                f_first = f_all[:, c % 2, :, 0:1]
                cs.link(nc.vector.tensor_tensor(f_first, f_first, keep[:, c:c + 1].unsqueeze(1).to_broadcast([P, KD, 1]), ALU.mult))

            def scan_up(c, *levels):
                f_c, s_c = f_all[:, c % 2], state[:, c % 2]
                for g in levels:
                    blocks = s_c[:, :, 1:1 + CH].rearrange("p m (i g) -> p m i g", g=g)
                    f_blocks = f_c.rearrange("p m (i g) -> p m i g", g=g)
                    c_left, c_right = blocks[:, :, :, g // 2 - 1], blocks[:, :, :, g - 1]
                    f_left, f_right = f_blocks[:, :, :, g // 2 - 1], f_blocks[:, :, :, g - 1]
                    t_g = tmp[:, :, 0:CH // g]
                    link(c, nc.vector.tensor_tensor(t_g, c_left, c_right, ALU.subtract))
                    link(c, nc.vector.tensor_tensor(t_g, t_g, f_right, ALU.mult))
                    nc.vector.tensor_tensor(f_right, f_right, f_left, ALU.mult)
                    link(c, nc.vector.tensor_tensor(c_right, c_right, t_g, ALU.add))

            def scan_down(c, *levels):
                f_c, s_c = f_all[:, c % 2], state[:, c % 2]
                for g in levels:
                    if g > CH:
                        c_here, f_here, h_before = s_c[:, :, CH:CH + 1], f_c[:, :, CH - 1:CH], s_c[:, :, 0:1]
                    else:
                        c_here = s_c[:, :, 1:1 + CH].rearrange("p m (i g) -> p m i g", g=g)[:, :, :, g // 2 - 1]
                        f_here = f_c.rearrange("p m (i g) -> p m i g", g=g)[:, :, :, g // 2 - 1]
                        h_before = s_c[:, :, 0:CH].rearrange("p m (i g) -> p m i g", g=g)[:, :, :, 0]
                    t_g = tmp[:, :, 0:max(CH // g, 1)]
                    link(c, nc.vector.tensor_tensor(t_g, h_before, c_here, ALU.subtract))
                    link(c, nc.vector.tensor_tensor(t_g, t_g, f_here, ALU.mult))
                    last = nc.vector.tensor_tensor(c_here, c_here, t_g, ALU.add)
                    if g > 2:
                        link(c, last)
                    else:
                        last.then_inc(states_ready, 1)

            def scan_end(c):
                assert tree["steps"] == TREE
                dve.wait_ge(states_ready, c + 1)
                cs.link(nc.vector.tensor_copy(state[:, (c + 1) % 2, :, 0:1], state[:, c % 2, :, CH:CH + 1]))

            def gated(c):
                lag = 2
                for m in range(KD + lag):
                    if m < KD:
                        if m == 0:
                            dve.wait_ge(r_ready, KD * (c + 1))
                        r, h = r_all[:, c % 2, m, :], state[:, c % 2, m, 1:1 + CH]
                        nc.vector.scalar_tensor_tensor(out=r, in0=h, scalar=scale64[:, m:m + 1], in1=r, op0=ALU.mult, op1=ALU.mult).then_inc(p_ready, 1)
                    if m >= lag:
                        dve.wait_ge(phi_ready, KD * c + m - lag + 1)
                        r = r_all[:, c % 2, m - lag, :]
                        nc.vector.tensor_tensor(pT[LO][:, m - lag, :], r, pT[HI][:, m - lag, :], ALU.subtract).then_inc(plo_ready, 1)

            def rms_scale(c):
                dve.wait_ge(rms_done, c + 1)
                cn.start(c)
                cn.link(nc.vector.tensor_scalar(col["ms"][:], wps[:, 0, 0:TPC], 1.0 / D, EPS, ALU.mult, ALU.add))
                nc.vector.tensor_scalar(rs["r"][:], col["ms"][:], UNSCALE**-2, None, ALU.mult).then_inc(rms_var, 1)

            def x1_tile(c, t):
                row = rows[:, TPC * c + t, 0:D]
                dve.wait_ge(rms_rstd, c + 1)
                dve.wait_ge(wo_done, TPC * c + t + 1)
                nc.vector.scalar_tensor_tensor(out=row, in0=wo_bank(t), scalar=rs["r"][:, t:t + 1], in1=row,
                                               op0=ALU.mult, op1=ALU.add).then_inc(x1_ready, 1)

            def x1_statistics(c, t):
                row = rows[:, TPC * c + t, :]
                dve.wait_ge(x1_ready, TPC * c + t + 1)
                wait(dve, nrm["b"]["xn"], TPC * (c - 1) + t + 1)
                statistics("b", t, 1, lambda i: row[:, 0:D], row[:, MEAN:MEAN + 2].unsqueeze(1))

            def rstd_payload(c):
                dve.wait_ge(nrm["b"]["rstd"], TPC * (c + 1))
                cn.link(nc.vector.tensor_copy(payload(c, RSTD), rs["b"][:]))
                cn.end()

            def payload(c, what):
                return rows[:, TPC * c:TPC * c + TPC, what]

            def each(a):
                return a[:].unsqueeze(2).to_broadcast([P, TPC, E])

            def route(c):
                d, eq = small["d"], small["eq"]
                cg.start(c)
                dve.wait_ge(logits_done, c + 1)
                cg.link(nc.vector.tensor_copy(small["lg"][:], sps[:, 0, 32:32 + TPC * E].rearrange("p (t e) -> p t e", e=E)))
                cg.link(nc.vector.tensor_reduce(col["max"][:], small["lg"][:], AX_X, ALU.max))
                nc.vector.tensor_tensor(d[:], small["lg"][:], each(col["max"]), ALU.subtract).then_inc(diff_ready, 1)
                dve.wait_ge(diff_ready, c + 1)
                cg.link(nc.vector.scalar_tensor_tensor(out=eq[:], in0=d[:], scalar=0.0, in1=rank[:], op0=ALU.is_ge, op1=ALU.mult))
                cg.link(nc.vector.tensor_reduce(col["m8"][:], eq[:], AX_X, ALU.max))
                nc.vector.tensor_tensor(onehot[:], rank[:], each(col["m8"]), ALU.is_equal).then_inc(onehot_ready, 1)

            def place(c):
                sg, om, rc, ex, pm = (small[n] for n in ("sg", "om", "rc", "ex", "pm"))
                dve.wait_ge(onehot_ready, c + 1)
                dve.wait_ge(sig_ready, c + 1)
                cg.link(nc.vector.tensor_scalar(om[:], sg[:], -1.0, 1.0, ALU.mult, ALU.add))
                cg.link(nc.vector.reciprocal(rc[:], om[:]))
                cg.link(nc.vector.scalar_tensor_tensor(out=ex[:], in0=sg[:], scalar=1.0, in1=rc[:], op0=ALU.add, op1=ALU.mult))
                cg.link(nc.vector.tensor_reduce(col["sum"][:], ex[:], AX_X, ALU.add))
                cg.link(nc.vector.reciprocal(col["gate"][:], col["sum"][:]))
                cg.link(nc.vector.tensor_scalar(payload(c, GATE), col["gate"][:], UNSCALE, None, ALU.mult))
                cg.step(nc.vector.tensor_scalar(col["slot"][:], col["m8"][:], -float(CAP), float(E * CAP), ALU.mult, ALU.add))
                dve.wait_ge(pos_done, c + 1)
                cg.link(nc.vector.tensor_tensor(pm[:], sps[:, 0, 64:64 + TPC * E].rearrange("p (t e) -> p t e", e=E), onehot[:], ALU.mult))
                cg.link(nc.vector.tensor_reduce(col["pos"][:], pm[:], AX_X, ALU.add))
                cg.step(nc.vector.tensor_scalar(col["over"][:], col["pos"][:], float(CAP), float(NOWHERE), ALU.is_ge, ALU.mult))
                cg.link(nc.vector.tensor_tensor(col["where"][:], col["slot"][:], col["pos"][:], ALU.add))
                nc.vector.tensor_tensor(slot_ids[:, TPC * c:TPC * c + TPC], col["where"][:], col["over"][:], ALU.add).then_inc(slots_ready, 1)
                cg.link(nc.vector.tensor_reduce(chunk_count[:], onehot[:].rearrange("p t e -> p e t"), AX_X, ALU.add))
                cg.link(nc.vector.tensor_tensor(before[:], before[:], chunk_count[:], ALU.add))
                cg.end()

            def w1_lo(e, js):
                for j in js:
                    if first(e) and j == NP // 2:
                        dve.wait_ge(lo_split, splits_before(0, "w1") + NP // 2)
                    split_lo(wA[HI][:, SLOT * j:SLOT * j + SLOT], wA[LO][:, SLOT * j:SLOT * j + SLOT], raw[:, j, :],
                             splits_before(e, "w1") + j + 1)

            t_statistics(0)
            t_statistics(1)
            first_xn(0)
            first_xn(1)
            first_lo(0)
            first_xn(2)
            first_lo(1)
            first_xn(3)
            first_lo(2)
            first_lo(3)
            for n in range(6):
                attn_weights(n)
            dve.wait_ge(small_in, 32)
            nc.vector.tensor_scalar(scale64[:], scale_in[:], WSCALE, None, ALU.mult).then_inc(small_split, 1)
            dve.wait_ge(small_split, 1)
            dve.wait_ge(consts, 1)
            for part in range(2, len(X_PARTS)):
                t_statistics(part)
            attn_weights(6)
            attn_weights(7)
            scan_start(0)
            scan_up(0, 2, 4, 8, 16, 32, 64, 128, 256, CH)
            scan_down(0, 2 * CH, CH, 256, 128, 64, 32, 16, 8, 4, 2)
            scan_end(0)
            gated(0)
            rms_scale(0)
            for c in range(1, NCH):
                scan_start(c)
                scan_up(c, 2, 4, 8)
                x1_statistics(c - 1, 0)
                scan_up(c, 16, 32)
                x1_statistics(c - 1, 1)
                scan_up(c, 64, 128)
                x1_statistics(c - 1, 2)
                scan_up(c, 256, CH)
                x1_statistics(c - 1, 3)
                scan_down(c, 2 * CH, CH, 256, 128, 64, 32, 16)
                rstd_payload(c - 1)
                scan_down(c, 8, 4)
                if c < NCH - 1:
                    route(c - 1)
                scan_down(c, 2)
                scan_end(c)
                gated(c)
                rms_scale(c)
                if c == NCH - 1:
                    route(c - 1)
                place(c - 1)
            for t in range(TPC):
                x1_tile(NCH - 1, t)
                x1_statistics(NCH - 1, t)
            w1_lo(0, range(NP // 2, NP))
            rstd_payload(NCH - 1)
            route(NCH - 1)
            place(NCH - 1)

            def e_normalise(e):
                for t in range(CT):
                    row = tile_at(CT * e + t)
                    wait(dve, nrm["e"]["lo"], CT * e)
                    nc.vector.tensor_scalar(xn[:, t, :], row[:, 0:D], row[:, MEAN:MEAN + 1], row[:, RSTD:RSTD + 1],
                                            ALU.subtract, ALU.mult).then_inc(nrm["e"]["xn"], 1)
                for t in range(CT):
                    dve.wait_ge(nrm["e"]["hi"], CT * e + t + 1)
                    nc.vector.tensor_tensor(xs[:, t, LO, :], xn[:, t, :], xs[:, t, HI, :], ALU.subtract).then_inc(nrm["e"]["lo"], 1)

            def combine(e, t):
                row = tile_at(CT * e + t)
                wait(dve, rows_out[t], 16 * e)
                nc.vector.tensor_copy(row_ids[:, t:t + 1], row[:, ID:ID + 1].bitcast(U32)).then_inc(ids_ready, 1)
                dve.wait_ge(down_done, CT * e + t + 1)
                dve.wait_ge(ids_ready, CT * e + t + 1)
                nc.vector.scalar_tensor_tensor(out=done_rows[:, t, :], in0=wps[:, t, :], scalar=row[:, GATE:GATE + 1], in1=row[:, 0:D],
                                               op0=ALU.mult, op1=ALU.add).then_inc(combined, 1)

            def expert(e, last):
                for j in range(NP):
                    dve.wait_ge(gel_ready, NP * e + j + 1)
                    g = gel[:, j % 2, :].rearrange("p (a n) -> p a n", a=2)
                    nc.vector.tensor_scalar(hid[:, HI, 2 * j:2 * j + 2, :], g, WSCALE, None, ALU.mult).then_inc(hhi_ready, 1)
                    split_lo(wB[HI][:, SLOT * j:SLOT * j + SLOT], wB[LO][:, SLOT * j:SLOT * j + SLOT], raw[:, j, :],
                             splits_before(e, "w2") + j + 1)
                    dve.wait_ge(hhi_ready, NP * e + j + 1)
                    nc.vector.scalar_tensor_tensor(out=hid[:, LO, 2 * j:2 * j + 2, :], in0=g, scalar=WSCALE, in1=hid[:, HI, 2 * j:2 * j + 2, :],
                                                   op0=ALU.mult, op1=ALU.subtract).then_inc(hlo_ready, 1)
                if not last:
                    e_normalise(e + 1)
                    w1_lo(e + 1, range(NP // 2))
                combine(e, 0)
                if not last:
                    w1_lo(e + 1, range(NP // 2, NP))
                combine(e, 1)

            dve.wait_ge(e_first, 16)
            e_normalise(0)
            dve.wait_ge(e_rest, 16)
            expert(0, False)
            with dve.Fori(1, E - 1) as e:
                expert(e, False)
            expert(E - 1, True)

        @block.tensor
        def _(pe):
            def turn(part, u, tiles, free, some=None):
                for t in some or range(tiles):
                    pe.wait_ge(nrm[part]["lo"], tiles * u + t + 1)
                    free(t)
                    for hl in range(2):
                        for k in range(KD):
                            last = nc.tensor.transpose(tps16[:, t % 2, hl, k, :], xs[:, t, hl, k * P:(k + 1) * P], ident[:])
                    last.then_inc(nrm[part]["turned"], 1)

            def part_t(c, *some):
                def free(t):
                    if t >= 2:
                        pe.wait_ge(nrm["t"]["copied"], TPC * c + t - 1)
                    elif not first(c):
                        pe.wait_ge(nrm["t"]["copied"], TPC * c)
                        wait(pe, nrm["b"]["copied"], TPC * (c - 2))
                turn("t", c, TPC, free, some)

            def project(c, w, m, done):
                n = 0
                for k in range(KD):
                    for a, b in PASSES:
                        last = nc.tensor.matmul(zps[:, w, :], proj[a][:, w, k, m * P:(m + 1) * P],
                                                xT[:, c % 2, b, k, :],
                                                start=(n == 0), stop=(n == 3 * KD - 1))
                        n += 1
                last.then_inc(done, 1)

            def z_f(c, m):
                if first(c) and m == 0:
                    pe.wait_ge(lo_split, 2)
                if m == 0:
                    pe.wait_ge(nrm["t"]["copied"], TPC * (c + 1))
                wait(pe, f_ready, KD * c + m)
                project(c, 0, m, zf_done)

            def z_c(c, m):
                if first(c) and m == 0:
                    pe.wait_ge(lo_split, 4)
                wait(pe, c_ready, KD * c + m)
                project(c, 1, m, zc_done)

            def z_r(c, m):
                if first(c) and m == 0:
                    pe.wait_ge(lo_split, 6)
                wait(pe, r_ready, KD * c + m)
                project(c, 2, m, zr_done)

            def sums_of_squares(c):
                pe.wait_ge(hsum_ready, c + 1)
                wait(pe, y_ready, TPC * c)
                for t in range(TPC):
                    last = nc.tensor.matmul(wps[:, 0, t:t + 1], hsq[:, 0, t * P:(t + 1) * P], ones32[:], start=True, stop=True)
                last.then_inc(rms_done, 1)

            def out_projection(c, *tiles):
                for t in tiles:
                    if t == 0:
                        pe.wait_ge(plo_ready, KD * (c + 1))
                        pe.wait_ge(lo_split, RING)
                    wait(pe, x1_ready if c == NCH - 1 and t >= 2 else y_ready, TPC * c + t - 1)
                    if t == 1:
                        pe.wait_ge(rms_var, c + 1)
                    n = 0
                    for m in range(KD):
                        for a, b in PASSES:
                            last = nc.tensor.matmul(wo_bank(t), pT[a][:, m, t * P:(t + 1) * P], proj[b][:, 3, m, :],
                                                    start=(n == 0), stop=(n == 3 * KD - 1))
                            n += 1
                    last.then_inc(wo_done, 1)

            def logits(c, *tiles):
                for t in tiles:
                    pe.wait_ge(nrm["b"]["copied"], TPC * c + t + 1)
                    if t == 0:
                        wait(pe, slots_ready, c)
                    for k in range(KD):
                        last = nc.tensor.matmul(sps[:, 0, 32 + t * E:32 + (t + 1) * E], x1T[:, t % 2, k, :], wg_in[:, k, :],
                                                start=(k == 0), stop=(k == KD - 1))
                    if t == TPC - 1:
                        last.then_inc(logits_done, 1)

            def turn_x1(c, *tiles):
                for t in tiles:
                    pe.wait_ge(nrm["b"]["xn"], TPC * c + t + 1)
                    wait(pe, nrm["b"]["copied"], TPC * c + t - 1)
                    if t < 2:
                        pe.wait_ge(nrm["t"]["copied"], TPC * min(c + 3, NCH))
                    for k in range(KD):
                        last = nc.tensor.transpose(tps32[:, t % 2, k, :], x1n[:, t, k * P:(k + 1) * P], ident32[:])
                    last.then_inc(nrm["b"]["turned"], 1)

            def positions(c):
                pe.wait_ge(onehot_ready, c + 1)
                wait(pe, chain_g, ROUTING * c)
                pos = sps[:, 0, 64:64 + TPC * E].rearrange("p (t e) -> p t e", e=E)
                nc.tensor.matmul(pos, earlier[:], onehot[:], start=True, stop=False)
                for t in range(TPC - 1):
                    nc.tensor.matmul(pos[:, t + 1:TPC, :], ones16[:], onehot[:, t:t + 1, :].to_broadcast([P, TPC - 1 - t, E]), start=False, stop=False)
                nc.tensor.matmul(pos, ones16[:], before[:].unsqueeze(1).to_broadcast([P, TPC, E]), start=False, stop=True).then_inc(pos_done, 1)

            def z(c, *ms):
                for m in ms:
                    z_f(c, m)
                    z_c(c, m)
                    z_r(c, m)

            pe.wait_ge(consts, 1)
            pe.wait_ge(small_in, 32)
            part_t(0)
            z(0, 0, 1)
            part_t(1, 0, 1)
            z_f(0, 2)
            part_t(1, 2, 3)
            z_c(0, 2)
            z_r(0, 2)
            z(0, 3)
            z(1, 0, 1)
            part_t(2, 0, 1)
            z_f(1, 2)
            part_t(2, 2, 3)
            z_c(1, 2)
            z_r(1, 2)
            z(1, 3)
            sums_of_squares(0)
            for c in range(2, NCH):
                out_projection(c - 2, 0, 1, 2, 3)
                z(c, 0)
                turn_x1(c - 2, 0, 1)
                z_f(c, 1)
                logits(c - 2, 0, 1)
                turn_x1(c - 2, 2, 3)
                z_c(c, 1)
                logits(c - 2, 2, 3)
                z_r(c, 1)
                if c + 1 < NCH:
                    part_t(c + 1, 0, 1)
                positions(c - 2)
                z_f(c, 2)
                if c + 1 < NCH:
                    part_t(c + 1, 2, 3)
                z_c(c, 2)
                z_r(c, 2)
                z_f(c, 3)
                sums_of_squares(c - 1)
                z_c(c, 3)
                z_r(c, 3)
            for c in range(NCH - 2, NCH):
                if c == NCH - 1:
                    sums_of_squares(c)
                out_projection(c, 0)
                if c == NCH - 1:
                    positions(c - 1)
                out_projection(c, 1, 2)
                if c == NCH - 1:
                    turn_x1(c, 0)
                out_projection(c, 3)
                if c < NCH - 1:
                    turn_x1(c, 0)
                turn_x1(c, 1)
                logits(c, 0)
                turn_x1(c, 2)
                logits(c, 1, 2)
                turn_x1(c, 3)
                logits(c, 3)
            positions(NCH - 1)

            def turn_expert(e):
                if first(e):
                    turn("e", e, CT, lambda t: None)
                else:
                    turn("e", e, CT, lambda t: pe.wait_ge(nrm["e"]["copied"], CT * e))

            def up(e, j):
                pe.wait_ge(lo_split, splits_before(e, "w1") + j + 1)
                if j == 0:
                    pe.wait_ge(nrm["e"]["copied"], CT * (e + 1))
                wait(pe, gel_ready, NP * e + (j - 1 if j < 2 else j - 2))
                for f in range(2):
                    n = 0
                    for k in range(KD):
                        for a, b in PASSES:
                            last = nc.tensor.matmul(zps[:, j % 3, f * CAP:(f + 1) * CAP], w1s[a][:, j, k, f * P:(f + 1) * P], xTe[:, b, k, :],
                                                    start=(n == 0), stop=(n == 3 * KD - 1))
                            n += 1
                last.then_inc(up_done, 1)

            def down(e, t):
                wait(pe, combined, CT * (e - 1) + t + 1)
                n = 0
                for j in range(NP):
                    if t == 0:
                        pe.wait_ge(lo_split, splits_before(e, "w2") + j + 1)
                        pe.wait_ge(hlo_ready, NP * e + j + 1)
                    for f in range(2):
                        for a, b in PASSES:
                            last = nc.tensor.matmul(wps[:, t, :], hid[:, a, 2 * j + f, t * P:(t + 1) * P], w2s[b][:, j, f, :],
                                                    start=(n == 0), stop=(n == 6 * NP - 1))
                            n += 1
                last.then_inc(down_done, 1)

            def expert(e, last):
                for j in range(NP):
                    up(e, j)
                down(e, 0)
                if not last:
                    turn_expert(e + 1)
                down(e, 1)

            turn_expert(0)
            expert(0, False)
            with pe.Fori(1, E - 1) as e:
                expert(e, False)
            expert(E - 1, True)


_INS = ["L0_attn_x", "L0_attn_Wr", "L0_attn_Wf", "L0_attn_Wc", "L0_attn_Wo", "L0_attn_ln_scale", "L0_ffn_w_gate", "L0_ffn_w1", "L0_ffn_w2"]
_OUTS = [((2, 1024, 512), "float32")]


def kernel(**inputs):
    import numpy as _np
    import concourse.bacc as _bacc
    from concourse import mybir as _mybir
    from concourse.bass_utils import run_bass_kernel_spmd as _run

    nc = _bacc.Bacc("TRN2", target_bir_lowering=False, num_devices=1)
    arrays, args = {}, []
    for name in _INS:
        a = _np.ascontiguousarray(inputs[name])
        arrays[f"in_{name}_dram"] = a
        args.append(nc.dram_tensor(f"in_{name}_dram", a.shape, _mybir.dt.from_np(a.dtype), kind="ExternalInput").ap())
    for i, (shape, dtype) in enumerate(_OUTS):
        dt = _mybir.dt.from_np(_np.dtype(dtype))
        args.append(nc.dram_tensor(f"out_{i}_dram", shape, dt, kind="ExternalOutput").ap())
    recurrent_block_with_experts(nc, *args)
    r = _run(nc, [arrays], core_ids=[0])
    return r.results[0]["out_0_dram"]
```
